# Optimizing a Trainium2 kernel written in Bass

```python
import numpy as np
import jax
import jax.numpy as jnp

def _softmax(x, axis=-1):
    return jax.nn.softmax(x, axis=axis)

def _gelu(x):
    return jax.nn.gelu(x, approximate=True)

def _silu(x):
    return jax.nn.silu(x)

def _sigmoid(x):
    return jax.nn.sigmoid(x)

def _layernorm(x, axis=-1, eps=1e-05):
    m = jnp.mean(x, axis=axis, keepdims=True)
    v = jnp.var(x, axis=axis, keepdims=True)
    return (x - m) / jnp.sqrt(v + eps)

def _scatter_add(tgt, idx, src, axis=0):
    return tgt.at[idx].add(src)

def _segment_sum(src, seg, n):
    return jax.ops.segment_sum(src, seg, n)
kernel_name = 'mk_gnn_preln_d2_gnn_r32_10fe89'

def setup_inputs(seed: int=0):
    np.random.seed(seed)
    _w = jnp.asarray

    def _rec_inputs():
        import jax
        import jax.numpy as jnp
        _gk = jax.random.key(seed)
        x = -0.000202 + 1 * jax.random.normal(jax.random.fold_in(_gk, 1), (50000, 128), jnp.float32)
        src = jax.random.randint(jax.random.fold_in(_gk, 2), (50000,), 0, 50000, jnp.int32)
        dst = jax.random.randint(jax.random.fold_in(_gk, 3), (50000,), 0, 50000, jnp.int32)
        _o = jnp.argsort(dst, stable=True)
        src = src[_o]
        dst = dst[_o]
        edge_attr_64 = 0.000135552 + 1.00015 * jax.random.normal(jax.random.fold_in(_gk, 12), (50000, 64), jnp.float32)
        return (x, src, dst, edge_attr_64)
    x, src, dst, edge_attr_64 = _rec_inputs()

    def _L0_gnn_setup():
        import jax, jax.numpy as jnp
        import numpy as np
        import math
        N, D_IN, H, C = (50000, 128, 4, 32)
        E = 25000
        key = jax.random.key(seed)
        ks = jax.random.split(key, 12)
        s = 0.05
        inp = {'x': jax.random.normal(ks[0], (N, D_IN), dtype=jnp.float32), 'edge_index': jax.random.randint(ks[1], (2, E), 0, N, dtype=jnp.int32), 'Wq': jax.random.normal(ks[2], (D_IN, H * C), dtype=jnp.float32) * s, 'bq': jax.random.normal(ks[3], (H * C,), dtype=jnp.float32) * s, 'Wk': jax.random.normal(ks[4], (D_IN, H * C), dtype=jnp.float32) * s, 'bk': jax.random.normal(ks[5], (H * C,), dtype=jnp.float32) * s, 'Wv': jax.random.normal(ks[6], (D_IN, H * C), dtype=jnp.float32) * s, 'bv': jax.random.normal(ks[7], (H * C,), dtype=jnp.float32) * s, 'Wskip': jax.random.normal(ks[8], (D_IN, H * C), dtype=jnp.float32) * s, 'bskip': jax.random.normal(ks[9], (H * C,), dtype=jnp.float32) * s}
        return inp
    _L0_gnn_all = _L0_gnn_setup()
    _L0_gnn_in = {k: v for k, v in _L0_gnn_all.items() if k in ('Wq', 'bq', 'Wk', 'bk', 'Wv', 'bv', 'Wskip', 'bskip')}
    del _L0_gnn_all

    def _L1_gnn_setup():
        import jax, jax.numpy as jnp
        import numpy as np
        N_NODES = 50000
        N_EDGES = 25000
        D_FEAT = 128
        D_EDGE = 64
        EMBED = 128
        key = jax.random.key(seed)
        ks = jax.random.split(key, 6)
        node_features = jax.random.normal(ks[0], (N_NODES, D_FEAT), dtype=jnp.float32)
        senders = jax.random.randint(ks[1], (N_EDGES,), 0, N_NODES)
        receivers = jax.random.randint(ks[2], (N_EDGES,), 0, N_NODES)
        edge_features = jax.random.normal(ks[3], (N_EDGES, D_EDGE), dtype=jnp.float32)
        W_kernel = jax.random.normal(ks[4], (D_FEAT, 2 * EMBED), dtype=jnp.float32) * (2.0 / (D_FEAT + 2 * EMBED)) ** 0.5
        W_bias = jnp.zeros((2 * EMBED,), dtype=jnp.float32)
        We_kernel = jax.random.normal(ks[5], (D_EDGE, EMBED), dtype=jnp.float32) * (2.0 / (D_EDGE + EMBED)) ** 0.5
        We_bias = jnp.zeros((EMBED,), dtype=jnp.float32)
        return dict(node_features=node_features, senders=senders, receivers=receivers, edge_features=edge_features, W_kernel=W_kernel, W_bias=W_bias, We_kernel=We_kernel, We_bias=We_bias)
    _L1_gnn_all = _L1_gnn_setup()
    _L1_gnn_in = {k: v for k, v in _L1_gnn_all.items() if k in ('W_kernel', 'W_bias', 'We_kernel', 'We_bias')}
    del _L1_gnn_all
    return {'x': x, 'src': src, 'dst': dst, 'edge_attr_64': edge_attr_64, 'L0_gnn_Wq': _L0_gnn_in['Wq'], 'L0_gnn_bq': _L0_gnn_in['bq'], 'L0_gnn_Wk': _L0_gnn_in['Wk'], 'L0_gnn_bk': _L0_gnn_in['bk'], 'L0_gnn_Wv': _L0_gnn_in['Wv'], 'L0_gnn_bv': _L0_gnn_in['bv'], 'L0_gnn_Wskip': _L0_gnn_in['Wskip'], 'L0_gnn_bskip': _L0_gnn_in['bskip'], 'L1_gnn_W_kernel': _L1_gnn_in['W_kernel'], 'L1_gnn_W_bias': _L1_gnn_in['W_bias'], 'L1_gnn_We_kernel': _L1_gnn_in['We_kernel'], 'L1_gnn_We_bias': _L1_gnn_in['We_bias']}

def reference(x, src, dst, edge_attr_64, L0_gnn_Wq, L0_gnn_bq, L0_gnn_Wk, L0_gnn_bk, L0_gnn_Wv, L0_gnn_bv, L0_gnn_Wskip, L0_gnn_bskip, L1_gnn_W_kernel, L1_gnn_W_bias, L1_gnn_We_kernel, L1_gnn_We_bias):
    import jax
    import jax.numpy as jnp

    def _L0_gnn_ref(x, edge_index, Wq, bq, Wk, bk, Wv, bv, Wskip, bskip):
        import jax, jax.numpy as jnp
        import numpy as np
        import math
        N, D_IN, H, C = (50000, 128, 4, 32)
        E = 25000
        n = x.shape[0]
        q = (x @ Wq + bq).reshape(n, H, C)
        k = (x @ Wk + bk).reshape(n, H, C)
        v = (x @ Wv + bv).reshape(n, H, C)
        src, dst = (edge_index[0], edge_index[1])
        alpha = jnp.einsum('ehc,ehc->eh', q[dst], k[src]) / math.sqrt(C)
        amax = jax.ops.segment_max(alpha, dst, num_segments=n)
        ea = jnp.exp(alpha - amax[dst])
        denom = jax.ops.segment_sum(ea, dst, num_segments=n)
        alpha = ea / (denom[dst] + 1e-16)
        out = jax.ops.segment_sum(v[src] * alpha[:, :, None], dst, num_segments=n)
        out = out.reshape(n, H * C)
        out = out + (x @ Wskip + bskip)
        return out

    def _L1_gnn_ref(node_features, senders, receivers, edge_features, W_kernel, W_bias, We_kernel, We_bias):
        import jax, jax.numpy as jnp
        import numpy as np
        N_NODES = 50000
        N_EDGES = 25000
        D_FEAT = 128
        D_EDGE = 64
        EMBED = 128
        num_nodes = node_features.shape[-2]
        hW = node_features @ W_kernel + W_bias
        h_self, h = jnp.split(hW, 2, axis=-1)
        send_edges = h[senders]
        send_edges = send_edges + (edge_features @ We_kernel + We_bias)
        in_degree = jax.ops.segment_sum(jnp.ones_like(receivers), receivers, num_nodes).astype(jnp.float32)
        recv_degree = in_degree[receivers]
        send_edges = send_edges * jnp.clip(recv_degree, 1, None)[..., None]
        nodes = h_self + jax.ops.segment_sum(send_edges, receivers, num_nodes)
        return nodes
    edge_index = jnp.stack([src, dst])
    h = jnp.maximum(_layernorm(x, axis=-1), 0.0)
    x = x + _L0_gnn_ref(h, edge_index, L0_gnn_Wq, L0_gnn_bq, L0_gnn_Wk, L0_gnn_bk, L0_gnn_Wv, L0_gnn_bv, L0_gnn_Wskip, L0_gnn_bskip)
    h = jnp.maximum(_layernorm(x, axis=-1), 0.0)
    x = x + _L1_gnn_ref(h, src, dst, edge_attr_64, L1_gnn_W_kernel, L1_gnn_W_bias, L1_gnn_We_kernel, L1_gnn_We_bias)
    return x

_drawn_inputs = setup_inputs


def setup_inputs(seed=0):
    import zlib

    import numpy as np

    out = dict(_drawn_inputs(seed))
    spreads = {'L1_gnn_W_bias': (0.0, 0.1), 'L1_gnn_We_bias': (0.0, 0.1)}
    factors = {'L0_gnn_Wq': 8.0, 'L0_gnn_bq': 29.984, 'L0_gnn_Wk': 8.0, 'L0_gnn_bk': 64.0}
    for name, (base, spread) in spreads.items():
        noise = np.random.default_rng([zlib.crc32(name.encode()), seed]).standard_normal(out[name].shape)
        drawn = base * np.exp(spread * noise) if base else spread * noise
        out[name] = jnp.asarray(drawn.astype(out[name].dtype))
    for name, factor in factors.items():
        out[name] = (out[name] * factor).astype(out[name].dtype)
    return out
```

```python
from contextlib import ExitStack

import numpy as np

import concourse.bass as bass
from concourse import mybir
from concourse.alu_op_type import AluOpType as ALU

F32 = mybir.dt.float32
BF16 = mybir.dt.bfloat16
I32 = mybir.dt.int32
ACT = mybir.ActivationFunctionType
AX_X = mybir.AxisListType.X

N, D, E, HEADS, DE = 50000, 128, 50000, 4, 64
CH = D // HEADS
NODES = 100
TILES = N // NODES
WIN = 128
B = 10
BATCHES = TILES // B
PAIRS = B // 2
BH = B * HEADS
EPS = 1e-5
BIG = 3.0e38
SCALE = 1.0 / float(np.sqrt(CH))
ROWS = 125
EROWS = E // ROWS
TG = TILES // ROWS

RSQRT_BITS = float(0x5F3759DF)
NEWTON = 3
N_IDX, N_SEG, N_STAT, N_TILE, N_MID, N_FIN = 4, 3, 4 + 3 * NEWTON, 3 * PAIRS, 4, 4 * PAIRS
N_OUT = 3 * PAIRS

STAT_STEPS = N_STAT + 1
T_DVE = (STAT_STEPS + 8, STAT_STEPS + 6)
T_ACT = (3, 2)
T_PE = (2, 2)
C_DVE = (STAT_STEPS + 16, STAT_STEPS + 4)
C_ACT = (4, 2)
C_PE = (5, 2)
NEVER = 2.0 * TILES


class Batch:

    def __init__(self, off, i=None):
        self.off, self.i = off, i

    def plus(self, n):
        return Batch(self.off + n, self.i)

    @property
    def par(self):
        return self.off % 2

    @property
    def known(self):
        return self.i is None

    def count(self, per, n):
        return self.off * per + n if self.known else self.i * (2 * per) + (self.off * per + n)

    def half(self, per, n):
        return (self.off // 2) * per + n if self.known else self.i * per + ((self.off // 2) * per + n)


def wait(eng, sem, value):
    if isinstance(value, int) and value <= 0:
        return
    eng.wait_ge(sem, value)


def pairs_ahead(k, j):
    return k.plus(j // PAIRS), j % PAIRS


def exists(k):
    return not k.known or 0 <= k.off < BATCHES


def steps(eng, body, first, last):
    inner = first + 3
    rounds = (last - 2 - inner) // 2
    for n in range(first, inner):
        body(Batch(n))
    with eng.Fori(0, rounds) as i:
        for n in (inner, inner + 1):
            body(Batch(n, i))
    for n in range(inner + 2 * rounds, last + 1):
        body(Batch(n))


def build(nc, x, edges, ea, Wq, bq, Wk, bk, Wv, bv, Ws, bs, W1, b1, We, be, out):
    x1 = nc.dram_tensor("x1_rows", (N, D), F32, kind="Internal").ap()
    starts_dram = nc.dram_tensor("window_starts", (2 * TG, ROWS), I32, kind="Internal").ap()

    with ExitStack() as ctx:
        def sb(name, shape, dt=F32):
            return ctx.enter_context(nc.sbuf_tensor("sb_" + name, shape, dt))

        def bank(name):
            return ctx.enter_context(nc.psum_tensor("ps_" + name, [128, 512], F32))

        def sem(name):
            return ctx.enter_context(nc.semaphore(name))

        ident = sb("ident", [128, 128])
        iota = sb("iota", [128, NODES])
        n0tab = sb("n0tab", [B, BATCHES])
        rep = sb("rep", [B, BH])
        ones = sb("ones", [128, 128])
        ones_b = sb("ones_b", [128, 128], BF16)
        w0 = sb("w0", [128, 4, D])
        w1 = sb("w1", [128, 2 * D])
        w1m = sb("w1m", [128, D + 4])
        weaug = sb("weaug", [128, D + 4])
        brow = sb("brow", [1, 6, D])
        berow = sb("berow", [1, D])
        bmsg = sb("bmsg", [1, D + 4])
        bres = sb("bres", [1, 2, 5 * D])
        bpart = sb("bpart", [1, 3, 5 * D], BF16)
        bsplit = sb("bsplit", [128, 5 * D], BF16)

        heads_i = sb("heads_i", [1, EROWS], I32)
        heads_f = sb("heads_f", [1, EROWS])
        thr = sb("thr", [ROWS, TG])
        cmp1 = sb("cmp1", [ROWS, TG, EROWS])
        cnt1 = sb("cnt1", [ROWS, TG])
        row_f = sb("row_f", [ROWS, TG])
        row_i = sb("row_i", [ROWS, TG], I32)
        row_e = sb("row_e", [ROWS, TG, 2 * ROWS], I32)
        cmp2 = sb("cmp2", [ROWS, TG, ROWS])
        cnt2 = sb("cnt2", [ROWS, TG])
        lo_f = sb("lo_f", [ROWS, TG])
        st_f = sb("st_f", [ROWS, 2 * TG])
        st_i = sb("st_i", [2 * TG, ROWS], I32)
        starts = sb("starts", [1, 2 * TILES + 1], I32)

        all_e = sb("all_e", [ROWS, 2 * EROWS], I32)
        next_e = sb("next_e", [ROWS, 1], I32)
        falls = sb("falls", [ROWS, EROWS])
        falls_any = sb("falls_any", [ROWS, 1])
        unsorted = sb("unsorted", [1, 3])
        tile_no = sb("tile_no", [1, TILES])
        zeros = sb("zeros", [1, TILES])
        run_len = sb("run_len", [1, TILES])
        is_long = sb("is_long", [1, TILES])
        later = sb("later", [1, TILES])
        later_min = sb("later_min", [1, TILES])
        chunk_lo = sb("chunk_lo", [1, TILES])
        chunk_hi = sb("chunk_hi", [1, TILES])
        long_count_f = sb("long_count_f", [1, 1])
        long_count = sb("long_count", [1, 1], I32)
        next_long = sb("next_long", [1, TILES], I32)
        first_chunk = sb("first_chunk", [1, TILES], I32)
        end_chunk = sb("end_chunk", [1, TILES], I32)

        n0all = sb("n0all", [128, TILES])
        chunk_e = sb("chunk_e", [ROWS, 2], I32)
        chunk_d = sb("chunk_d", [ROWS, 1])
        outside = sb("outside", [ROWS, NODES])
        masked = sb("masked", [ROWS, HEADS, NODES])
        acc = sb("acc", [NODES, D + HEADS])
        run_max = sb("run_max", [NODES, HEADS])
        chunk_max = sb("chunk_max", [NODES, HEADS])
        new_max = sb("new_max", [NODES, HEADS])
        max_step = sb("max_step", [NODES, HEADS])
        rescale = sb("rescale", [NODES, HEADS])

        rows_i = sb("rows_i", [B, 2, 2 * WIN], I32)
        rows_f = sb("rows_f", [B, 2, 2, WIN])
        src_idx = sb("src_idx", [128, 2, B], I32)
        src_all = sb("src_all", [128, TILES], I32)
        drel_all = sb("drel_all", [128, TILES])
        drep = sb("drep", [BH, WIN])
        dne = sb("dne", [BH, WIN - 1])
        segm = sb("segm", [BH, 2, WIN + 1])
        member = sb("member", [128, 2, B, NODES])
        memberT = sb("memberT", [NODES, B, WIN])
        xn = sb("xn", [NODES, 2, B, D])
        xs = sb("xs", [128, 2, B, D])
        st = sb("st", [128, 2, 2 * B, 6])
        ssum = sb("ssum", [128, 2 * B])
        sdif = sb("sdif", [128, 2 * B])
        svar = sb("svar", [128, 2 * B])
        sd2 = sb("sd2", [128, 2 * B])
        sv2 = sb("sv2", [128, 2 * B])
        var = sb("var", [128, 2 * B])
        guess = sb("guess", [128, 2, 2 * B], I32)
        nwt = sb("nwt", [128, 2, 2 * B])
        rstd = sb("rstd", [128, 2, 2 * B])
        shift = sb("shift", [128, 2, 2 * B])
        hn = sb("hn", [NODES, 2, 2, D])
        hs = sb("hs", [128, 2, 2, D])
        hT = sb("hT", [128, 2, 2, 2, 128])
        qkv = sb("qkv", [128, 2, B, 3 * D])
        prod = sb("prod", [128, 2, D])
        alpha = sb("alpha", [128, 2, 128])
        fmax = sb("fmax", [BH, WIN])
        smax = sb("smax", [BH, WIN])
        dl = sb("dl", [128, BH])
        vw = sb("vw", [128, 2, B, D + 4])
        xsk = sb("xsk", [NODES, 2, B, D])
        den = sb("den", [NODES, 2, HEADS])
        rden = sb("rden", [NODES, 2, HEADS])
        att = sb("att", [NODES, 2, D])
        xo = sb("xo", [NODES, 2, B, D])
        eaw = sb("eaw", [128, 2, B, 128])
        aggT = sb("aggT", [128, 2, 3, NODES])
        yself = sb("yself", [NODES, 2, D])
        deg = sb("deg", [NODES, 2, 1])

        banks = [bank(f"b{n}") for n in range(8)]
        ps_hT, ps_qkv = banks[0:2], banks[2:4]
        ps_dv, ps_misc, ps_agg, ps_mT = banks[4], banks[5], banks[6], banks[7]
        ps_t1, ps_self, ps_msg = banks[0:2], banks[2:4], [banks[4], banks[6]]

        const_load = sem("const_load")
        const_made = sem("const_made")
        bias_step = sem("bias_step")
        bias_placed = sem("bias_placed")
        search = sem("search")
        heads_load = sem("heads_load")
        heads_spread = sem("heads_spread")
        rows_gather = sem("rows_gather")
        starts_turned = sem("starts_turned")
        starts_out = sem("starts_out")
        starts_in = sem("starts_in")
        zeroed = sem("zeroed")
        all_edges_load = sem("all_edges_load")
        list_step = sem("list_step")
        falls_summed = sem("falls_summed")
        long_done = [sem("L0_long_done"), sem("L1_long_done")]

        class Layer:

            def __init__(self, n):
                def s(name):
                    return sem(f"L{n}_{name}")
                self.win = [s("win_loaded0"), s("win_loaded1")]
                self.xn = [s("nodes_loaded0"), s("nodes_loaded1")]
                self.ea = [s("edge_feat_loaded0"), s("edge_feat_loaded1")]
                self.gat = [s("gathered0"), s("gathered1")]
                self.stored = [s("stored0"), s("stored1")]
                self.idx = s("idx_step")
                self.turned_idx = s("idx_turned")
                self.pair_free = s("pair_free")
                self.cols = s("gather_cols_ready")
                self.small_turn = s("small_turn_starts")
                self.member = s("member_built")
                self.bn = s("bn_stats_done")
                self.stat = s("stat_step")
                self.seg = s("segment_step")
                self.spread = s("rows_spread")
                self.shift = s("shift_ready")
                self.relu = s("relu_done")
                self.hT = s("h_turned")
                self.hT_sb = s("h_turned_copied")
                self.mT = s("member_turned")
                self.mT_sb = s("member_turned_copied")
                self.qkv = s("qkv_ready")
                self.qkv_sb = s("qkv_copied")
                self.dv = s("skip_and_qe_ready")
                self.tile = s("tile_step")
                self.aT = s("alpha_turned")
                self.maxT = s("max_turned")
                self.mid = s("mid_step")
                self.exp = s("exp_done")
                self.agg = s("agg_ready")
                self.fin = s("fin_step")

        class LongTiles:

            def __init__(self, n):
                def s(name):
                    return sem(f"L{n}_long_{name}")
                self.n = n
                self.rows = s("rows_loaded")
                self.edges = s("edges_loaded")
                self.feat = s("features_loaded")
                self.gathered = s("gathered")
                self.stored = s("stored")
                self.go = s("waits_over")
                self.dve_tile, self.act_tile, self.pe_tile = s("dve_tile"), s("act_tile"), s("pe_tile")
                self.dve, self.act, self.pe = s("dve_chunk"), s("act_chunk"), s("pe_chunk")
                self.first = {
                    "SP": [],
                    "Pool": [],
                    "DVE": [(self.dve_tile, T_DVE[n]), (self.dve, C_DVE[n])],
                    "Activation": [(self.act_tile, T_ACT[n]), (self.act, C_ACT[n])],
                    "PE": [(self.pe_tile, T_PE[n]), (self.pe, C_PE[n])],
                }

        L0, L1 = Layer(0), Layer(1)
        S0, S1 = LongTiles(0), LongTiles(1)
        block = ctx.enter_context(nc.Block())

        dst_rows = edges.rearrange("(r c) two -> r (c two)", c=ROWS)

        def long_tiles(eng, L, S, before, chunk, after):
            for p in range(2):
                eng.wait_ge(L.stored[p], 16 * (BATCHES // 2))
            eng.wait_ge(list_step, 12)
            count = eng.value_load(long_count[0:1, 0:1], min_val=0, max_val=TILES)
            cursor = eng.alloc_register(f"L{S.n}_cursor_{eng.engine.name}")
            chunks = eng.alloc_register(f"L{S.n}_chunks_{eng.engine.name}")
            eng.reg_mov(cursor, 0)
            eng.reg_mov(chunks, 1)
            for primed, by in S.first[eng.engine.name]:
                eng.sem_inc(primed, by)
            with eng.If(count > 0):
                with eng.Fori(1, count + 1) as i:
                    tile = eng.value_load(next_long[0:1, bass.ds(eng.snap(cursor), 1)], min_val=0, max_val=TILES - 1)
                    first = eng.value_load(first_chunk[0:1, bass.ds(tile, 1)], min_val=0, max_val=EROWS - 1)
                    end = eng.value_load(end_chunk[0:1, bass.ds(tile, 1)], min_val=1, max_val=EROWS)
                    if before:
                        before(i, tile, eng.snap(chunks))
                    with eng.Fori(first, end) as c:
                        if chunk:
                            chunk(c, tile, eng.snap(chunks))
                        eng.reg_add(chunks, chunks, 1)
                    if after:
                        after(i, tile, eng.snap(chunks))
                    eng.reg_mov(cursor, tile + 1)

        @block.sync
        def _(sp):
            for j, w in enumerate((Wq, Wk, Wv, Ws)):
                sp.dma_start(w0[:, j, :], w).then_inc(const_load, 16)
            sp.dma_start(w1[:], W1).then_inc(const_load, 16)
            sp.wait_ge(zeroed, 1)
            sp.dma_start(weaug[0:DE, 0:D], We).then_inc(const_load, 16)
            for j, b in enumerate((bq, bk, bv, bs)):
                sp.dma_start(brow[:, j, :], b.rearrange("(o n) -> o n", o=1)).then_inc(const_load, 16)
            sp.dma_start(brow[:, 4:6, :].rearrange("o j n -> o (j n)"),
                         b1.rearrange("(o n) -> o n", o=1)).then_inc(const_load, 16)
            sp.dma_start(berow[:], be.rearrange("(o n) -> o n", o=1)).then_inc(const_load, 16)
            with nc.allow_non_contiguous_dma(reason="400 words, once"):
                sp.dma_start(heads_i[:], edges.rearrange("(r c) two -> r c two", c=ROWS)[:, 0, 1:2]
                             .rearrange("r o -> o r")).then_inc(heads_load, 16)
            sp.dma_start(all_e[:], edges.rearrange("(r c) two -> r (c two)", c=EROWS)).then_inc(all_edges_load, 16)
            sp.wait_ge(list_step, 1)
            with nc.allow_non_contiguous_dma(reason="a word a partition, once"):
                sp.dma_start(next_e[0:ROWS - 1, :], edges.rearrange("(r c) two -> r c two", c=EROWS)[1:ROWS, 0, 1:2]
                             ).then_inc(all_edges_load, 16)
            sp.wait_ge(search, 9)
            sp.dma_start(starts_dram, st_i[:]).then_inc(starts_out, 16)
            sp.wait_ge(starts_out, 16)
            sp.dma_start(starts[0:1, 0:2 * TILES], starts_dram.rearrange("(o g) r -> o (g r)", o=1)
                         ).then_inc(starts_in, 16)
            sp.wait_ge(bias_step, 7)
            sp.dma_start(bsplit[0:3, :], bpart[0:1, :, :]).then_inc(bias_placed, 16)
            sp.dma_start(weaug[DE:DE + 1, :], bmsg[:]).then_inc(bias_placed, 16)
            sp.wait_ge(starts_in, 16)

            def windows(k):
                p = k.par
                wait(sp, L0.idx, k.plus(-2).count(N_IDX, 2))
                sp.wait_ge(starts_in, 16)
                for t in range(B):
                    start = sp.value_load(starts[0:1, bass.ds(k.count(B, t), 1)], min_val=0, max_val=E - WIN)
                    sp.dma_start(rows_i[t:t + 1, p, :],
                                 edges[bass.ds(start, WIN), :].rearrange("(o e) two -> o (e two)", o=1)
                                 ).then_inc(L0.win[p], 16)

            def features(k):
                p = k.par
                wait(sp, L1.agg, k.plus(-2).count(B, B))
                sp.wait_ge(starts_in, 16)
                for t in range(B):
                    start = sp.value_load(starts[0:1, bass.ds(k.count(B, t), 1)], min_val=0, max_val=E - WIN)
                    sp.dma_start(eaw[:, p, t, 0:DE], ea[bass.ds(start, WIN), :]).then_inc(L1.ea[p], 16)

            def nodes(L, k, table):
                p = k.par
                wait(sp, L.tile, k.plus(-2).count(N_TILE, N_TILE))
                rows = table[bass.ds(k.count(B * NODES, 0), B * NODES), :]
                sp.dma_start(xn[:, p, :, :], rows.rearrange("(t n) d -> n t d", n=NODES)).then_inc(L.xn[p], 16)

            def store(L, k, table, done_sem, per):
                p = k.par
                sp.wait_ge(done_sem, k.count(per, per))
                rows = table[bass.ds(k.count(B * NODES, 0), B * NODES), :]
                sp.dma_start(rows.rearrange("(t n) d -> n t d", n=NODES), xo[:, p, :, :]).then_inc(L.stored[p], 16)

            def step(L, table, to, done, per, k):
                if exists(k.plus(1)):
                    nodes(L, k.plus(1), table)
                    if L is L1:
                        features(k.plus(1))
                if L is L0 and exists(k.plus(3)):
                    windows(k.plus(3))
                if exists(k.plus(-1)):
                    store(L, k.plus(-1), to, done, per)

            windows(Batch(0))
            nodes(L0, Batch(0), x)
            windows(Batch(1))
            windows(Batch(2))
            steps(sp, lambda k: step(L0, x, x1, L0.fin, N_FIN, k), 0, BATCHES)

            def long_rows(L, S, table):
                def before(i, tile, n):
                    sp.wait_ge(S.dve_tile, i * T_DVE[S.n])
                    sp.sem_inc(S.go, 1)
                    sp.dma_start(xn[:, 0, 0, :], table[bass.ds(tile * NODES, NODES), :]).then_inc(S.rows, 16)
                return before

            def long_edges(S):
                def chunk(c, tile, n):
                    sp.wait_ge(S.dve, n * C_DVE[S.n])
                    sp.sem_inc(S.go, 1)
                    sp.dma_start(chunk_e[:], edges[bass.ds(c * ROWS, ROWS), :]).then_inc(S.edges, 16)
                    if S is S1:
                        sp.dma_start(eaw[0:ROWS, 0, 0, 0:DE], ea[bass.ds(c * ROWS, ROWS), :]).then_inc(S.feat, 16)
                return chunk

            def long_store(S, to):
                def after(i, tile, n):
                    sp.wait_ge(S.dve_tile, i * T_DVE[S.n] + T_DVE[S.n])
                    sp.sem_inc(S.go, 1)
                    sp.dma_start(to[bass.ds(tile * NODES, NODES), :], xo[:, 0, 0, :]).then_inc(S.stored, 16)
                    sp.wait_ge(S.stored, i * 16)
                    sp.sem_inc(S.go, 1)
                return after

            long_tiles(sp, L0, S0, long_rows(L0, S0, x), long_edges(S0), long_store(S0, x1))
            sp.sem_inc(long_done[0], 1)
            sp.wait_ge(long_done[0], 1)
            nodes(L1, Batch(0), x1)
            features(Batch(0))
            steps(sp, lambda k: step(L1, x1, out, L1.tile, N_OUT, k), 0, BATCHES)
            long_tiles(sp, L1, S1, long_rows(L1, S1, x1), long_edges(S1), long_store(S1, out))

        @block.gpsimd
        def _(pool):
            pool.memset(ones[:], 1.0).then_inc(const_made, 1)
            pool.memset(ident[:], 0.0).then_inc(const_made, 1)
            pool.memset(rep[:], 0.0).then_inc(const_made, 1)
            pool.iota(iota[:], pattern=[[1, NODES]], base=0, channel_multiplier=0,
                      allow_small_or_imprecise_dtypes=True).then_inc(const_made, 1)
            pool.iota(n0tab[:], pattern=[[B * NODES, BATCHES]], base=0, channel_multiplier=NODES,
                      allow_small_or_imprecise_dtypes=True).then_inc(const_made, 1)
            pool.iota(thr[:], pattern=[[ROWS * NODES, TG]], base=0, channel_multiplier=NODES,
                      allow_small_or_imprecise_dtypes=True).then_inc(const_made, 1)
            pool.iota(tile_no[:], pattern=[[1, TILES]], base=0, channel_multiplier=0,
                      allow_small_or_imprecise_dtypes=True).then_inc(const_made, 1)
            pool.iota(n0all[:], pattern=[[NODES, TILES]], base=0, channel_multiplier=0,
                      allow_small_or_imprecise_dtypes=True).then_inc(const_made, 1)
            pool.wait_ge(const_made, 8)
            pool.affine_select(out=ident[:], in_=ident[:], compare_op=ALU.not_equal, fill=1.0, base=0,
                               pattern=[[-1, 128]], channel_multiplier=1).then_inc(const_made, 1)
            pool.affine_select(out=rep[:].rearrange("p (t h) -> p t h", h=HEADS),
                               in_=rep[:].rearrange("p (t h) -> p t h", h=HEADS),
                               compare_op=ALU.not_equal, fill=1.0, base=0,
                               pattern=[[-1, B], [0, HEADS]], channel_multiplier=1).then_inc(const_made, 1)
            pool.wait_ge(search, 4)
            for g in range(TG):
                pool.indirect_dma_start(out=row_e[:, g, :], out_offset=None, in_=dst_rows,
                                        in_offset=bass.IndirectOffsetOnAxis(ap=row_i[:, g:g + 1], axis=0)
                                        ).then_inc(rows_gather, 16)

            def gathers(L, k, table):
                p = k.par
                pool.wait_ge(L.cols, k.count(1, 1))
                for t in range(B):
                    if t % 2 == 0:
                        wait(pool, L.relu, k.plus(-2).count(2 * B, 2 * t + 4))
                        pool.sem_inc(L.pair_free, 1)
                    pool.indirect_dma_start(out=xs[:, p, t, :], out_offset=None, in_=table,
                                            in_offset=bass.IndirectOffsetOnAxis(ap=src_idx[:, p, t:t + 1], axis=0)
                                            ).then_inc(L.gat[p], 16)

            def long_gather(S, table):
                def chunk(c, tile, n):
                    pool.wait_ge(S.edges, n * 16)
                    pool.wait_ge(S.act, n * C_ACT[S.n])
                    pool.sem_inc(S.go, 1)
                    pool.indirect_dma_start(out=xs[0:ROWS, 0, 0, :], out_offset=None, in_=table,
                                            in_offset=bass.IndirectOffsetOnAxis(ap=chunk_e[:, 0:1], axis=0)
                                            ).then_inc(S.gathered, 16)
                return chunk

            steps(pool, lambda k: gathers(L0, k, x), 0, BATCHES - 1)
            long_tiles(pool, L0, S0, None, long_gather(S0, x), None)
            pool.wait_ge(long_done[0], 1)
            steps(pool, lambda k: gathers(L1, k, x1), 0, BATCHES - 1)
            long_tiles(pool, L1, S1, None, long_gather(S1, x1), None)

        @block.vector
        def _(dve):
            dve.memset(next_e[:], E).then_inc(list_step, 1)
            dve.memset(weaug[:], 0.0).then_inc(zeroed, 1)
            dve.memset(bsplit[:], 0.0).then_inc(zeroed, 1)
            dve.memset(ones_b[:], 1.0).then_inc(zeroed, 1)
            dve.memset(w1m[:], 0.0).then_inc(zeroed, 1)
            dve.memset(bmsg[:], 0.0).then_inc(zeroed, 1)
            dve.memset(st[:], 0.0).then_inc(zeroed, 1)
            dve.memset(hT[:], 0.0).then_inc(zeroed, 1)
            dve.memset(alpha[:], 0.0).then_inc(zeroed, 1)
            dve.memset(segm[:, :, 0:WIN + 1:WIN], -BIG).then_inc(zeroed, 1)
            dve.memset(eaw[:], 0.0).then_inc(zeroed, 1)
            dve.wait_ge(zeroed, 10)
            dve.memset(eaw[:, :, :, DE:DE + 1], 1.0).then_inc(zeroed, 1)

            dve.wait_ge(heads_load, 16)
            dve.tensor_copy(heads_f[:], heads_i[:]).then_inc(search, 1)
            dve.wait_ge(heads_spread, 1)
            dve.wait_ge(const_made, 10)
            for g in range(TG):
                ins = dve.tensor_scalar(cmp1[:, g, :], ps_misc[0:ROWS, 0:EROWS], thr[:, g:g + 1], None, ALU.is_lt)
            ins.then_inc(search, 1)
            dve.wait_ge(search, 2)
            dve.tensor_reduce(cnt1[:], cmp1[:], AX_X, ALU.add).then_inc(search, 1)
            dve.wait_ge(search, 3)
            dve.tensor_scalar(row_f[:], cnt1[:], -1.0, 0.0, ALU.add, ALU.max)
            dve.tensor_scalar(row_i[:], cnt1[:], -1.0, 0.0, ALU.add, ALU.max).then_inc(search, 1)
            dve.wait_ge(rows_gather, 16 * TG)
            for g in range(TG):
                ins = dve.tensor_scalar(cmp2[:, g, :], row_e[:, g, 1::2], thr[:, g:g + 1], None, ALU.is_lt)
            ins.then_inc(search, 1)
            dve.wait_ge(search, 5)
            dve.tensor_reduce(cnt2[:], cmp2[:], AX_X, ALU.add).then_inc(search, 1)
            dve.wait_ge(search, 6)
            dve.scalar_tensor_tensor(lo_f[:], row_f[:], float(ROWS), cnt2[:], ALU.mult, ALU.add).then_inc(search, 1)
            dve.wait_ge(search, 7)
            dve.tensor_scalar(st_f[:, 0:TG], lo_f[:], float(E - WIN), None, ALU.min)
            dve.tensor_copy(st_f[:, TG:2 * TG], lo_f[:]).then_inc(search, 1)
            dve.wait_ge(starts_turned, 1)
            dve.tensor_copy(st_i[:], ps_misc[0:2 * TG, 0:ROWS]).then_inc(search, 1)

            dve.wait_ge(all_edges_load, 32)
            dve.tensor_tensor(falls[:, 0:EROWS - 1], all_e[:, 3::2], all_e[:, 1:2 * EROWS - 1:2], ALU.is_lt)
            dve.tensor_tensor(falls[:, EROWS - 1:EROWS], next_e[:], all_e[:, 2 * EROWS - 1:2 * EROWS], ALU.is_lt
                              ).then_inc(list_step, 1)
            dve.wait_ge(list_step, 2)
            dve.tensor_reduce(falls_any[:], falls[:], AX_X, ALU.max).then_inc(list_step, 1)
            dve.memset(zeros[:], 0.0)
            dve.memset(starts[0:1, 2 * TILES:2 * TILES + 1], E)

            dve.wait_ge(const_load, 16 * 12)
            flat = brow[:].rearrange("o j n -> o (j n)")[:, 0:5 * D]
            dve.tensor_copy(bpart[:, 0, :], flat).then_inc(bias_step, 1)
            dve.wait_ge(bias_step, 1)
            dve.tensor_tensor(bres[:, 0, :], flat, bpart[:, 0, :], ALU.subtract).then_inc(bias_step, 1)
            dve.wait_ge(bias_step, 2)
            dve.tensor_copy(bpart[:, 1, :], bres[:, 0, :]).then_inc(bias_step, 1)
            dve.wait_ge(bias_step, 3)
            dve.tensor_tensor(bres[:, 1, :], bres[:, 0, :], bpart[:, 1, :], ALU.subtract).then_inc(bias_step, 1)
            dve.wait_ge(bias_step, 4)
            dve.tensor_copy(bpart[:, 2, :], bres[:, 1, :]).then_inc(bias_step, 1)
            dve.tensor_tensor(bmsg[:, 0:D], brow[:, 5, :], berow[:], ALU.add).then_inc(bias_step, 1)
            dve.memset(bmsg[:, D:D + 1], 1.0).then_inc(bias_step, 1)
            dve.tensor_copy(w1m[:, 0:D], w1[:, D:2 * D]).then_inc(bias_step, 1)

            def list_long_tiles():
                lo = starts[0:1, TILES:2 * TILES]
                hi = starts[0:1, TILES + 1:2 * TILES + 1]
                dve.wait_ge(starts_in, 16)
                dve.tensor_tensor(run_len[:], hi, starts[0:1, 0:TILES], ALU.subtract)
                dve.tensor_scalar(chunk_lo[:], lo, 1.0 / ROWS, -1.0, ALU.mult, ALU.add)
                dve.tensor_scalar(chunk_hi[:], hi, 1.0 / ROWS, 2.0, ALU.mult, ALU.add)
                dve.wait_ge(falls_summed, 1)
                dve.tensor_scalar(unsorted[:, 0:1], ps_mT[0:1, 0:1], 1.0, None, ALU.min).then_inc(list_step, 1)
                dve.wait_ge(list_step, 4)
                dve.tensor_scalar(unsorted[:, 1:2], unsorted[:, 0:1], -1.0, 1.0, ALU.mult, ALU.add)
                dve.tensor_scalar(unsorted[:, 2:3], unsorted[:, 0:1], float(EROWS), None, ALU.mult)
                dve.tensor_scalar(is_long[:], run_len[:], float(WIN), unsorted[:, 0:1], ALU.is_gt, ALU.max
                                  ).then_inc(list_step, 1)
                dve.wait_ge(list_step, 5)
                dve.tensor_scalar(first_chunk[:], chunk_lo[:], 0.0, unsorted[:, 1:2], ALU.max, ALU.mult)
                dve.tensor_scalar(end_chunk[:], chunk_hi[:], unsorted[:, 2:3], float(EROWS), ALU.max, ALU.min
                                  ).then_inc(list_step, 1)
                dve.tensor_reduce(long_count_f[:], is_long[:], AX_X, ALU.add).then_inc(list_step, 1)
                dve.tensor_scalar(later[:], is_long[:], -NEVER, NEVER, ALU.mult, ALU.add).then_inc(list_step, 1)
                dve.wait_ge(list_step, 8)
                dve.tensor_copy(long_count[:], long_count_f[:]).then_inc(list_step, 1)
                dve.tensor_tensor(later[:], later[:], tile_no[:], ALU.add).then_inc(list_step, 1)
                dve.wait_ge(list_step, 10)
                dve.tensor_tensor_scan(later_min[:, ::-1], zeros[:, ::-1], later[:, ::-1], 2 * NEVER,
                                       ALU.add, ALU.min).then_inc(list_step, 1)
                dve.wait_ge(list_step, 11)
                dve.tensor_scalar(next_long[:], later_min[:], float(TILES - 1), None, ALU.min).then_inc(list_step, 1)

            def idx_rows(k):
                p = k.par
                dve.wait_ge(L0.win[p], k.half(16 * B, 16 * B))
                wait(dve, L0.turned_idx, k.plus(-2).count(1, 1))
                wait(dve, L0.spread, k.plus(-2).count(1, 1))
                pairs = rows_i[:, p, :].rearrange("b (e two) -> b e two", two=2)
                dve.tensor_copy(rows_f[:, p, 0, :], pairs[:, :, 0]).then_inc(L0.idx, 1)
                dve.tensor_scalar(rows_f[:, p, 1, :], pairs[:, :, 1], n0tab[:, bass.ds(k.count(1, 0), 1)], None,
                                  ALU.subtract).then_inc(L0.idx, 1)

            def idx_cols(k):
                dve.wait_ge(L0.turned_idx, k.count(1, 1))
                cols = bass.ds(k.count(B, 0), B)
                dve.tensor_copy(src_all[:, cols], ps_misc[:, 0:B]).then_inc(L0.idx, 1)
                dve.tensor_copy(drel_all[:, cols], ps_misc[:, B:2 * B]).then_inc(L0.idx, 1)

            def gather_cols(L, k):
                dve.wait_ge(L0.idx, k.count(N_IDX, 3))
                wait(dve, L.gat[k.par], k.half(16 * B, 0))
                dve.tensor_scalar(src_idx[:, k.par, :], src_all[:, bass.ds(k.count(B, 0), B)], 0, None, ALU.add
                                  ).then_inc(L.cols, 1)

            def segment_mask(k):
                p = k.par
                dve.wait_ge(L0.spread, k.count(1, 1))
                wait(dve, L0.seg, k.plus(-1).count(N_SEG, N_SEG))
                dve.tensor_copy(drep[:], ps_misc[0:BH, 0:WIN]).then_inc(L0.seg, 1)
                dve.wait_ge(L0.seg, k.count(N_SEG, 1))
                dve.tensor_tensor(dne[:], drep[:, 1:WIN], drep[:, 0:WIN - 1], ALU.not_equal).then_inc(L0.seg, 1)
                dve.wait_ge(L0.seg, k.count(N_SEG, 2))
                dve.tensor_scalar(segm[:, p, 1:WIN], dne[:], -BIG, None, ALU.mult).then_inc(L0.seg, 1)

            def members(L, k, used_sem, used):
                p = k.par
                dve.wait_ge(L0.idx, k.count(N_IDX, 4))
                wait(dve, used_sem, used)
                dve.tensor_tensor(member[:, p, :, :], drel_all[:, bass.ds(k.count(B, 0), B)].unsqueeze(2).to_broadcast([128, B, NODES]),
                                  iota[:].unsqueeze(1).to_broadcast([128, B, NODES]), ALU.is_equal
                                  ).then_inc(L.member, 1)

            def source_stats(L, k, first, last):
                p = k.par
                if first == 0:
                    dve.wait_ge(L.gat[p], k.half(16 * B, 16 * B))
                    wait(dve, L.stat, k.plus(-2).count(N_STAT, 1))
                for t in range(first, last):
                    ins = dve.bn_stats(st[:, p, B + t, :], xs[:, p, t, :])
                if last == B:
                    ins.then_inc(L.bn, 1)

            def node_stats(L, k):
                p = k.par
                dve.wait_ge(L.xn[p], k.half(16, 16))
                for t in range(B):
                    ins = dve.bn_stats(st[0:NODES, p, t, :], xn[:, p, t, :])
                ins.then_inc(L.bn, 1)

            def stat_math(n, p, c):
                if n == 0:
                    dve.tensor_tensor(ssum[:, c], st[:, p, c, 1], st[:, p, c, 4], ALU.add)
                    dve.tensor_tensor(sdif[:, c], st[:, p, c, 1], st[:, p, c, 4], ALU.subtract)
                    return dve.tensor_tensor(svar[:, c], st[:, p, c, 2], st[:, p, c, 5], ALU.add)
                if n == 1:
                    dve.scalar_tensor_tensor(sd2[:, c], sdif[:, c], 0.25, sdif[:, c], ALU.mult, ALU.mult)
                    return dve.tensor_scalar(sv2[:, c], svar[:, c], 1.0 / D, EPS, ALU.mult, ALU.add)
                if n == 2:
                    return dve.tensor_tensor(var[:, c], sd2[:, c], sv2[:, c], ALU.add)
                if n == 3:
                    return dve.tensor_scalar(guess[:, 0, c], var[:, c].bitcast(I32), -0.5, RSQRT_BITS,
                                             ALU.mult, ALU.add)
                if n == N_STAT:
                    return dve.scalar_tensor_tensor(shift[:, p, c], ssum[:, c], -0.5, rstd[:, p, c],
                                                    ALU.mult, ALU.mult)
                m = (n - 4) // 3
                y = guess[:, m % 2, c].bitcast(F32)
                if (n - 4) % 3 == 0:
                    return dve.tensor_tensor(nwt[:, 0, c], y, y, ALU.mult)
                if (n - 4) % 3 == 1:
                    return dve.scalar_tensor_tensor(nwt[:, 1, c], nwt[:, 0, c], -0.5, var[:, c], ALU.mult, ALU.mult)
                better = guess[:, (m + 1) % 2, c].bitcast(F32) if m < NEWTON - 1 else rstd[:, p, c]
                return dve.scalar_tensor_tensor(better, nwt[:, 1, c], 1.5, y, ALU.add, ALU.mult)

            def stat_step(L, k, n):
                if n == 0:
                    dve.wait_ge(L.bn, k.count(2, 2))
                    wait(dve, L.shift, k.plus(-1).count(1, 1))
                else:
                    dve.wait_ge(L.stat, k.count(N_STAT, n))
                if n == N_STAT - 1:
                    wait(dve, L.relu, k.plus(-2).count(2 * B, 2 * B))
                stat_math(n, k.par, slice(0, 2 * B)).then_inc(L.shift if n == N_STAT else L.stat, 1)

            def all_stats(L, k):
                source_stats(L, k, 0, B)
                node_stats(L, k)
                for n in range(N_STAT + 1):
                    stat_step(L, k, n)

            def segment_max(k):
                p = k.par
                dve.wait_ge(L0.aT, k.count(1, 1))
                wait(dve, L0.maxT, k.plus(-1).count(1, 1))
                dve.tensor_tensor_scan(fmax[:], segm[:, p, 0:WIN], ps_misc[0:BH, 0:WIN], -BIG, ALU.add, ALU.max
                                       ).then_inc(L0.mid, 1)
                dve.wait_ge(L0.mid, k.count(N_MID, 1))
                dve.tensor_tensor_scan(smax[:, ::-1], segm[:, p, 1:WIN + 1][:, ::-1], fmax[:, ::-1], -BIG,
                                       ALU.add, ALU.max).then_inc(L0.mid, 1)

            def below_max(k):
                p = k.par
                dve.wait_ge(L0.maxT, k.count(1, 1))
                wait(dve, L0.exp, k.plus(-1).count(1, 1))
                dve.tensor_tensor(dl[:], alpha[:, p, 0:BH], ps_misc[:, 0:BH], ALU.subtract).then_inc(L0.mid, 1)

            def weigh(k):
                p = k.par
                dve.wait_ge(L0.exp, k.count(1, 1))
                wait(dve, L0.agg, k.plus(-2).count(PAIRS, PAIRS))
                split = dict(h=HEADS)
                dve.tensor_tensor(vw[:, p, :, 0:D].rearrange("e t (h c) -> e t h c", **split),
                                  qkv[:, p, :, 2 * D:3 * D].rearrange("e t (h c) -> e t h c", **split),
                                  vw[:, p, :, D:D + HEADS].unsqueeze(3).to_broadcast([128, B, HEADS, CH]),
                                  ALU.mult).then_inc(L0.mid, 1)

            def pair_scores(k, j):
                p = k.par
                dve.wait_ge(L0.dv, k.count(PAIRS, j + 1))
                dve.wait_ge(L0.qkv_sb, k.count(B, 2 * j + 2))
                wait(dve, L0.tile, k.count(N_TILE, 3 * j))
                t2 = slice(2 * j, 2 * j + 2)
                dve.tensor_tensor(prod[:], ps_dv[:, 2 * D:4 * D].rearrange("e (t c) -> e t c", t=2),
                                  qkv[:, p, t2, D:2 * D], ALU.mult).then_inc(L0.tile, 1)
                if j == 0:
                    wait(dve, L0.fin, k.plus(-2).count(N_FIN, N_FIN))
                dve.tensor_tensor(xsk[:, p, t2, :], xn[:, p, t2, :],
                                  ps_dv[0:NODES, 0:2 * D].rearrange("e (t c) -> e t c", t=2), ALU.add
                                  ).then_inc(L0.tile, 1)
                dve.wait_ge(L0.tile, k.count(N_TILE, 3 * j + 1))
                if j == 0:
                    wait(dve, L0.mid, k.plus(-2).count(N_MID, 3))
                dve.tensor_reduce(alpha[:, p, 2 * HEADS * j:2 * HEADS * (j + 1)],
                                  prod[:].rearrange("e t (h c) -> e (t h) c", h=HEADS), AX_X, ALU.add
                                  ).then_inc(L0.tile, 1)

            def out_step(k, j, n):
                p = k.par
                t2 = slice(2 * j, 2 * j + 2)
                a = ps_agg[0:NODES, 0:2 * (D + 4)].rearrange("n (t c) -> n t c", t=2)
                if n == 0:
                    dve.wait_ge(L0.agg, k.count(PAIRS, j + 1))
                wait(dve, L0.fin, k.count(N_FIN, 4 * j + n))
                if n == 0:
                    dve.tensor_scalar(den[:], a[:, :, D:D + HEADS], 1e-16, None, ALU.add).then_inc(L0.fin, 1)
                elif n == 1:
                    dve.reciprocal(rden[:], den[:]).then_inc(L0.fin, 1)
                elif n == 2:
                    dve.tensor_tensor(att[:].rearrange("n t (h c) -> n t h c", h=HEADS),
                                      a[:, :, 0:D].rearrange("n t (h c) -> n t h c", h=HEADS),
                                      rden[:].unsqueeze(3).to_broadcast([NODES, 2, HEADS, CH]), ALU.mult
                                      ).then_inc(L0.fin, 1)
                else:
                    if j == 0:
                        wait(dve, L0.stored[p], k.half(16, 0))
                        dve.wait_ge(L0.tile, k.count(N_TILE, N_TILE))
                    dve.tensor_tensor(xo[:, p, t2, :], att[:], xsk[:, p, t2, :], ALU.add).then_inc(L0.fin, 1)

            def step0(k):
                this, prev, nxt, nxt2 = (exists(k.plus(n)) for n in (0, -1, 1, 2))

                def out_and_stats(j, first):
                    for n in range(4):
                        if prev:
                            out_step(k.plus(-1), j, n)
                        if nxt and first is not None and first + n <= N_STAT:
                            stat_step(L0, k.plus(1), first + n)

                if this:
                    segment_mask(k)
                if nxt2:
                    idx_rows(k.plus(2))
                if nxt:
                    source_stats(L0, k.plus(1), 0, 4)
                if nxt2:
                    idx_cols(k.plus(2))
                    gather_cols(L0, k.plus(2))
                if prev:
                    pair_scores(k.plus(-1), PAIRS - 1)
                if nxt:
                    source_stats(L0, k.plus(1), 4, B)
                if prev:
                    segment_max(k.plus(-1))
                if this:
                    pair_scores(k, 0)
                if prev:
                    below_max(k.plus(-1))
                if nxt:
                    node_stats(L0, k.plus(1))
                if prev:
                    weigh(k.plus(-1))
                if nxt:
                    stat_step(L0, k.plus(1), 0)
                if this:
                    pair_scores(k, 1)
                if nxt:
                    stat_step(L0, k.plus(1), 1)
                out_and_stats(0, 2)
                if this:
                    pair_scores(k, 2)
                out_and_stats(1, 6)
                out_and_stats(2, 10)
                if this:
                    pair_scores(k, 3)
                out_and_stats(3, None)
                out_and_stats(4, None)
                if nxt:
                    members(L0, k.plus(1), L0.agg, k.plus(-1).count(PAIRS, PAIRS))

            for n in range(2):
                idx_rows(Batch(n))
                idx_cols(Batch(n))
                gather_cols(L0, Batch(n))
            list_long_tiles()
            members(L0, Batch(0), L0.agg, 0)
            all_stats(L0, Batch(0))
            steps(dve, step0, 0, BATCHES)

            def sum_step(k, j, n):
                p, q = k.par, (k.par * PAIRS + j) % 2
                t2 = slice(2 * j, 2 * j + 2)
                a = ps_self[q][0:NODES, 0:2 * D].rearrange("n (t c) -> n t c", t=2)
                m = ps_msg[q][0:NODES, 0:2 * (D + 4)].rearrange("n (t c) -> n t c", t=2)
                if n == 0:
                    dve.wait_ge(L1.qkv, k.count(B, 2 * j + 2))
                    wait(dve, L1.tile, k.count(N_OUT, 3 * j))
                    dve.tensor_tensor(yself[:], xn[:, p, t2, :], a, ALU.add).then_inc(L1.tile, 1)
                elif n == 1:
                    dve.tensor_scalar(deg[:], m[:, :, D:D + 1], 1.0, None, ALU.max).then_inc(L1.tile, 1)
                else:
                    dve.wait_ge(L1.tile, k.count(N_OUT, 3 * j + 2))
                    if j == 0:
                        wait(dve, L1.stored[p], k.half(16, 0))
                    for t in range(2):
                        ins = dve.scalar_tensor_tensor(xo[:, p, 2 * j + t, :], m[:, t, 0:D], deg[:, t, :],
                                                       yself[:, t, :], ALU.mult, ALU.add)
                    ins.then_inc(L1.tile, 1)

            def step1(k):
                nxt, nxt2 = (exists(k.plus(n)) for n in (1, 2))

                def sums(j, first):
                    for n in range(3):
                        sum_step(k, j, n)
                        if nxt and first is not None:
                            stat_step(L1, k.plus(1), first + n)

                if nxt2:
                    gather_cols(L1, k.plus(2))
                if nxt:
                    source_stats(L1, k.plus(1), 0, 6)
                sums(0, None)
                if nxt:
                    source_stats(L1, k.plus(1), 6, B)
                if nxt:
                    node_stats(L1, k.plus(1))
                    stat_step(L1, k.plus(1), 0)
                sums(1, 1)
                if nxt:
                    stat_step(L1, k.plus(1), 4)
                    members(L1, k.plus(1), L1.agg, k.plus(-1).count(B, B))
                sums(2, 5)
                if nxt:
                    stat_step(L1, k.plus(1), 8)
                sums(3, 9)
                if nxt:
                    for n in range(12, N_STAT + 1):
                        stat_step(L1, k.plus(1), n)
                sums(4, None)

            def long_node_stats(S):
                def before(i, tile, n):
                    base = i * T_DVE[S.n]
                    dve.wait_ge(S.rows, i * 16)
                    dve.bn_stats(st[0:NODES, 0, 0, :], xn[:, 0, 0, :]).then_inc(S.dve_tile, 1)
                    for m in range(STAT_STEPS):
                        dve.wait_ge(S.dve_tile, base + (1 + m))
                        stat_math(m, 0, slice(0, 1)).then_inc(S.dve_tile, 1)
                    dve.memset(acc[:], 0.0).then_inc(S.dve_tile, 1)
                    dve.memset(run_max[:], -BIG).then_inc(S.dve_tile, 1)
                    dve.wait_ge(S.pe_tile, i * T_PE[S.n] + 2)
                    if S is S0:
                        ins = dve.tensor_tensor(xsk[:, 0, 0, :], xn[:, 0, 0, :], ps_dv[0:NODES, 0:D], ALU.add)
                    else:
                        ins = dve.tensor_tensor(yself[:, 0, :], xn[:, 0, 0, :], ps_self[0][0:NODES, 0:D], ALU.add)
                    ins.then_inc(S.dve_tile, 1)
                return before

            def long_members(S, tile, n):
                base = n * C_DVE[S.n]
                dve.wait_ge(S.edges, n * 16)
                dve.tensor_scalar(chunk_d[:], chunk_e[:, 1:2], n0all[0:ROWS, bass.ds(tile, 1)], None, ALU.subtract
                                  ).then_inc(S.dve, 1)
                dve.wait_ge(S.dve, base + 1)
                dve.tensor_scalar(member[0:ROWS, 0, 0, :], iota[0:ROWS, :], chunk_d[:], None, ALU.is_equal
                                  ).then_inc(S.dve, 1)

            def long_source_stats(S, n, first):
                base = n * C_DVE[S.n] + first
                dve.wait_ge(S.gathered, n * 16)
                dve.bn_stats(st[0:ROWS, 0, 1, :], xs[0:ROWS, 0, 0, :]).then_inc(S.dve, 1)
                for m in range(STAT_STEPS):
                    dve.wait_ge(S.dve, base + (1 + m))
                    stat_math(m, 0, slice(1, 2)).then_inc(S.dve, 1)

            def long_chunk0(c, tile, n):
                S, base = S0, n * C_DVE[0] + (STAT_STEPS + 4)
                long_members(S, tile, n)
                dve.wait_ge(S.dve, n * C_DVE[0] + 2)
                dve.tensor_scalar(outside[:], member[0:ROWS, 0, 0, :], -1.0, BIG, ALU.add, ALU.mult).then_inc(S.dve, 1)
                long_source_stats(S, n, 3)
                dve.wait_ge(S.act, n * C_ACT[0] + 3)
                dve.tensor_tensor(prod[0:ROWS, 0, :], ps_dv[0:ROWS, 0:D], qkv[0:ROWS, 0, 0, D:2 * D], ALU.mult
                                  ).then_inc(S.dve, 1)
                dve.wait_ge(S.dve, base + 1)
                dve.tensor_reduce(alpha[0:ROWS, 0, 0:HEADS], prod[0:ROWS, 0, :].rearrange("e (h c) -> e h c", h=HEADS),
                                  AX_X, ALU.add).then_inc(S.dve, 1)
                dve.wait_ge(S.dve, base + 2)
                for h in range(HEADS):
                    ins = dve.scalar_tensor_tensor(masked[:, h, :], member[0:ROWS, 0, 0, :], alpha[0:ROWS, 0, h:h + 1],
                                                   outside[:], ALU.mult, ALU.add)
                ins.then_inc(S.dve, 1)
                dve.wait_ge(S.pe, n * C_PE[0] + 3)
                dve.tensor_reduce(chunk_max[:], ps_agg[0:NODES, 0:HEADS * ROWS].rearrange("n (h e) -> n h e", h=HEADS),
                                  AX_X, ALU.max).then_inc(S.dve, 1)
                dve.wait_ge(S.dve, base + 4)
                dve.tensor_tensor(new_max[:], run_max[:], chunk_max[:], ALU.max).then_inc(S.dve, 1)
                dve.wait_ge(S.dve, base + 5)
                dve.tensor_tensor(max_step[:], run_max[:], new_max[:], ALU.subtract).then_inc(S.dve, 1)
                dve.wait_ge(S.dve, base + 6)
                dve.tensor_copy(run_max[:], new_max[:]).then_inc(S.dve, 1)
                dve.wait_ge(S.pe, n * C_PE[0] + 4)
                dve.tensor_tensor(dl[0:ROWS, 0:HEADS], alpha[0:ROWS, 0, 0:HEADS], ps_misc[0:ROWS, 0:HEADS],
                                  ALU.subtract).then_inc(S.dve, 1)
                dve.wait_ge(S.dve, base + 8)
                dve.tensor_scalar(dl[0:ROWS, 0:HEADS], dl[0:ROWS, 0:HEADS], 0.0, None, ALU.min).then_inc(S.dve, 1)
                dve.wait_ge(S.act, n * C_ACT[0] + 4)
                dve.tensor_tensor(vw[0:ROWS, 0, 0, 0:D].rearrange("e (h c) -> e h c", h=HEADS),
                                  qkv[0:ROWS, 0, 0, 2 * D:3 * D].rearrange("e (h c) -> e h c", h=HEADS),
                                  vw[0:ROWS, 0, 0, D:D + HEADS].unsqueeze(2).to_broadcast([ROWS, HEADS, CH]),
                                  ALU.mult).then_inc(S.dve, 1)
                dve.tensor_tensor(acc[:, 0:D].rearrange("n (h c) -> n h c", h=HEADS),
                                  acc[:, 0:D].rearrange("n (h c) -> n h c", h=HEADS),
                                  rescale[:].unsqueeze(2).to_broadcast([NODES, HEADS, CH]), ALU.mult)
                dve.tensor_tensor(acc[:, D:D + HEADS], acc[:, D:D + HEADS], rescale[:], ALU.mult).then_inc(S.dve, 1)
                dve.wait_ge(S.dve, base + 11)
                dve.wait_ge(S.pe, n * C_PE[0] + 5)
                dve.tensor_tensor(acc[:], acc[:], ps_agg[0:NODES, 0:D + HEADS], ALU.add).then_inc(S.dve, 1)

            def long_finish0(i, tile, n):
                S, base = S0, i * T_DVE[0] + (STAT_STEPS + 4)
                dve.wait_ge(S.dve, n * C_DVE[0])
                dve.tensor_scalar(den[:, 0, :], acc[:, D:D + HEADS], 1e-16, None, ALU.add).then_inc(S.dve_tile, 1)
                dve.wait_ge(S.dve_tile, base + 1)
                dve.reciprocal(rden[:, 0, :], den[:, 0, :]).then_inc(S.dve_tile, 1)
                dve.wait_ge(S.dve_tile, base + 2)
                dve.tensor_tensor(att[:, 0, :].rearrange("n (h c) -> n h c", h=HEADS),
                                  acc[:, 0:D].rearrange("n (h c) -> n h c", h=HEADS),
                                  rden[:, 0, :].unsqueeze(2).to_broadcast([NODES, HEADS, CH]), ALU.mult
                                  ).then_inc(S.dve_tile, 1)
                dve.wait_ge(S.dve_tile, base + 3)
                dve.tensor_tensor(xo[:, 0, 0, :], att[:, 0, :], xsk[:, 0, 0, :], ALU.add).then_inc(S.dve_tile, 1)

            def long_chunk1(c, tile, n):
                long_members(S1, tile, n)
                long_source_stats(S1, n, 2)
                dve.wait_ge(S1.pe, n * C_PE[1] + 2)
                dve.tensor_tensor(acc[:], acc[:], ps_msg[0][0:NODES, 0:D + HEADS], ALU.add).then_inc(S1.dve, 1)

            def long_finish1(i, tile, n):
                dve.wait_ge(S1.dve, n * C_DVE[1])
                dve.tensor_scalar(deg[:, 0, :], acc[:, D:D + 1], 1.0, None, ALU.max).then_inc(S1.dve_tile, 1)
                dve.wait_ge(S1.dve_tile, i * T_DVE[1] + (STAT_STEPS + 5))
                dve.scalar_tensor_tensor(xo[:, 0, 0, :], acc[:, 0:D], deg[:, 0, :], yself[:, 0, :],
                                         ALU.mult, ALU.add).then_inc(S1.dve_tile, 1)

            long_tiles(dve, L0, S0, long_node_stats(S0), long_chunk0, long_finish0)
            dve.wait_ge(long_done[0], 1)
            for n in range(2):
                gather_cols(L1, Batch(n))
            members(L1, Batch(0), L1.agg, 0)
            all_stats(L1, Batch(0))
            steps(dve, step1, 0, BATCHES - 1)
            long_tiles(dve, L1, S1, long_node_stats(S1), long_chunk1, long_finish1)

        @block.scalar
        def _(act):
            def relu_pair(L, k, j, freed_sem, freed):
                p, q = k.par, (k.par * PAIRS + j) % 2
                if j == 0:
                    act.wait_ge(L.shift, k.count(1, 1))
                wait(act, freed_sem, freed)
                for t in range(2):
                    n = 2 * j + t
                    nc.scalar.activation(hn[:, q, t, :], xn[:, p, n, :], ACT.Relu,
                                         scale=rstd[0:NODES, p, n:n + 1], bias=shift[0:NODES, p, n:n + 1]
                                         ).then_inc(L.relu, 1)
                    nc.scalar.activation(hs[:, q, t, :], xs[:, p, n, :], ACT.Relu,
                                         scale=rstd[:, p, B + n:B + n + 1], bias=shift[:, p, B + n:B + n + 1]
                                         ).then_inc(L.relu, 1)

            def copy_hT(k, j):
                q = (k.par * PAIRS + j) % 2
                act.wait_ge(L0.hT, k.count(PAIRS, j + 1))
                wait(act, L0.dv, k.count(PAIRS, j - 1))
                src = ps_hT[q][:, :].rearrange("c (t s n) -> c t s n", t=2, s=2)
                nc.scalar.copy(hT[:, q, :, 0, 0:NODES], src[:, :, 0, 0:NODES])
                nc.scalar.copy(hT[:, q, :, 1, :], src[:, :, 1, :]).then_inc(L0.hT_sb, 1)

            def copy_qkv(k, j):
                p = k.par
                for t in range(2 * j, 2 * j + 2):
                    act.wait_ge(L0.qkv, k.count(B, t + 1))
                    if t == 0:
                        wait(act, L0.mid, k.plus(-2).count(N_MID, 4))
                    nc.scalar.copy(qkv[:, p, t, :], ps_qkv[t % 2][:, 0:3 * D]).then_inc(L0.qkv_sb, 1)

            def copy_memberT(k, g):
                t, n = 4 * g, min(4, B - 4 * g)
                act.wait_ge(L0.mT, k.count(3, g + 1))
                if g == 0:
                    wait(act, L0.dv, k.plus(-1).count(PAIRS, PAIRS))
                nc.scalar.copy(memberT[:, t:t + n, :],
                               ps_mT[0:NODES, 0:n * WIN].rearrange("n (t e) -> n t e", e=WIN)).then_inc(L0.mT_sb, 1)

            def exps(k):
                p = k.par
                act.wait_ge(L0.mid, k.count(N_MID, 3))
                wait(act, L0.agg, k.plus(-2).count(PAIRS, PAIRS))
                nc.scalar.activation(vw[:, p, :, D:D + HEADS], dl[:].rearrange("e (t h) -> e t h", h=HEADS),
                                     ACT.Exp, scale=SCALE).then_inc(L0.exp, 1)

            def step0(k):
                this, prev = exists(k), exists(k.plus(-1))
                for j in range(PAIRS):
                    ahead, a = pairs_ahead(k, j + 2)
                    if exists(ahead) and (this or a >= 2):
                        relu_pair(L0, ahead, a, L0.hT, ahead.count(PAIRS, a - 1))
                    if this and j == 0:
                        copy_memberT(k, 0)
                    ahead, a = pairs_ahead(k, j + 1)
                    if exists(ahead) and (this or a >= 1):
                        copy_hT(ahead, a)
                    if this and j == 0:
                        copy_memberT(k, 1)
                    if this:
                        copy_qkv(k, j)
                    if this and j == 0:
                        copy_memberT(k, 2)
                    if prev and j == 1:
                        exps(k.plus(-1))

            act.wait_ge(zeroed, 11)
            relu_pair(L0, Batch(0), 0, L0.hT, 0)
            copy_hT(Batch(0), 0)
            relu_pair(L0, Batch(0), 1, L0.hT, 0)
            steps(act, step0, 0, BATCHES)

            def copy_agg(k, t):
                act.wait_ge(L1.agg, k.count(B, t + 1))
                wait(act, L1.qkv, k.count(B, t - 1))
                nc.scalar.copy(aggT[:, t % 2, :, :],
                               ps_t1[t % 2][:, 0:3 * NODES].rearrange("c (s n) -> c s n", s=3)
                               ).then_inc(L1.hT_sb, 1)

            def step1(k):
                for j in range(PAIRS):
                    ahead, a = pairs_ahead(k, j + 2)
                    if exists(ahead):
                        relu_pair(L1, ahead, a, L1.agg, ahead.count(B, 2 * a - 2))
                    ahead, a = pairs_ahead(k, j + 1)
                    if exists(ahead):
                        copy_agg(ahead, 2 * a)
                        copy_agg(ahead, 2 * a + 1)

            def long_turned_rows(S):
                def before(i, tile, n):
                    act.wait_ge(S.dve_tile, i * T_DVE[S.n] + (1 + STAT_STEPS))
                    nc.scalar.activation(hn[:, 0, 0, :], xn[:, 0, 0, :], ACT.Relu, scale=rstd[0:NODES, 0, 0:1],
                                         bias=shift[0:NODES, 0, 0:1]).then_inc(S.act_tile, 1)
                    act.wait_ge(S.pe_tile, i * T_PE[S.n] + 1)
                    nc.scalar.copy(hT[:, 0, 0, 0, 0:NODES], ps_hT[0][:, 0:NODES]).then_inc(S.act_tile, 1)
                    if S is S0:
                        act.wait_ge(S.pe_tile, i * T_PE[0] + 2)
                        nc.scalar.copy(qkv[0:NODES, 0, 0, 0:D], ps_qkv[0][0:NODES, 0:D]).then_inc(S.act_tile, 1)
                return before

            def long_relu(S, n):
                act.wait_ge(S.dve, n * C_DVE[S.n] + (STAT_STEPS + 4 - S.n))
                nc.scalar.activation(hs[0:ROWS, 0, 0, :], xs[0:ROWS, 0, 0, :], ACT.Relu, scale=rstd[0:ROWS, 0, 1:2],
                                     bias=shift[0:ROWS, 0, 1:2]).then_inc(S.act, 1)

            def long_chunk0(c, tile, n):
                long_relu(S0, n)
                act.wait_ge(S0.pe, n * C_PE[0] + 1)
                nc.scalar.copy(hT[:, 0, 0, 1, 0:ROWS], ps_hT[0][:, 0:ROWS])
                nc.scalar.copy(memberT[:, 0, 0:ROWS], ps_mT[0:NODES, 0:ROWS]).then_inc(S0.act, 1)
                act.wait_ge(S0.pe, n * C_PE[0] + 2)
                nc.scalar.copy(qkv[0:ROWS, 0, 0, D:3 * D], ps_qkv[1][0:ROWS, 0:2 * D]).then_inc(S0.act, 1)
                act.wait_ge(S0.dve, n * C_DVE[0] + (STAT_STEPS + 4 + 9))
                nc.scalar.activation(rescale[:], max_step[:], ACT.Exp, scale=SCALE)
                nc.scalar.activation(vw[0:ROWS, 0, 0, D:D + HEADS], dl[0:ROWS, 0:HEADS], ACT.Exp, scale=SCALE
                                     ).then_inc(S0.act, 1)

            def long_chunk1(c, tile, n):
                long_relu(S1, n)
                act.wait_ge(S1.pe, n * C_PE[1] + 1)
                nc.scalar.copy(aggT[:, 0, 1:3, :], ps_t1[1][:, 0:2 * NODES].rearrange("c (s n) -> c s n", s=2)
                               ).then_inc(S1.act, 1)

            long_tiles(act, L0, S0, long_turned_rows(S0), long_chunk0, None)
            act.wait_ge(long_done[0], 1)
            relu_pair(L1, Batch(0), 0, L1.agg, 0)
            copy_agg(Batch(0), 0)
            copy_agg(Batch(0), 1)
            relu_pair(L1, Batch(0), 1, L1.agg, 0)
            steps(act, step1, 0, BATCHES - 1)
            long_tiles(act, L1, S1, long_turned_rows(S1), long_chunk1, None)

        @block.tensor
        def _(pe):
            pe.wait_ge(search, 1)
            pe.wait_ge(const_made, 10)
            nc.tensor.matmul(ps_misc[0:ROWS, 0:EROWS], ones[0:1, 0:ROWS], heads_f[:], start=True, stop=True
                             ).then_inc(heads_spread, 1)
            pe.wait_ge(search, 8)
            nc.tensor.transpose(ps_misc[0:2 * TG, 0:ROWS], st_f[:], ident[0:ROWS, 0:ROWS]).then_inc(starts_turned, 1)
            pe.wait_ge(list_step, 3)
            nc.tensor.matmul(ps_mT[0:1, 0:1], falls_any[:], ones[0:ROWS, 0:1], start=True, stop=True
                             ).then_inc(falls_summed, 1)
            pe.wait_ge(bias_placed, 32)
            pe.wait_ge(bias_step, 8)
            pe.wait_ge(const_load, 16 * 12)
            pe.wait_ge(search, 9)
            pe.wait_ge(zeroed, 11)

            def turn_idx(k):
                p = k.par
                pe.wait_ge(L0.idx, k.count(N_IDX, 2))
                wait(pe, L0.idx, k.plus(-1).count(N_IDX, N_IDX))
                wait(pe, L0.seg, k.plus(-2).count(N_SEG, 1))
                wait(pe, L0.mid, k.plus(-4).count(N_MID, 3))
                pe.sem_inc(L0.small_turn, 1)
                nc.tensor.transpose(ps_misc[:, 0:B], rows_f[:, p, 0, :], ident[0:B, 0:B])
                nc.tensor.transpose(ps_misc[:, B:2 * B], rows_f[:, p, 1, :], ident[0:B, 0:B]
                                    ).then_inc(L0.turned_idx, 1)

            def spread_rows(k):
                wait(pe, L0.mid, k.plus(-2).count(N_MID, 3))
                pe.wait_ge(L0.idx, k.plus(1).count(N_IDX, N_IDX) if exists(k.plus(1)) else
                           k.count(N_IDX, N_IDX))
                nc.tensor.matmul(ps_misc[0:BH, 0:WIN], rep[:], rows_f[:, k.par, 1, :], start=True, stop=True
                                 ).then_inc(L0.spread, 1)

            def turn_members(k, g):
                p, t = k.par, 4 * g
                if g == 0:
                    pe.wait_ge(L0.member, k.count(1, 1))
                wait(pe, L0.mT_sb, k.count(3, g))
                for n in range(min(4, B - t)):
                    last = nc.tensor.transpose(ps_mT[0:NODES, n * WIN:(n + 1) * WIN], member[:, p, t + n, :], ident[:])
                last.then_inc(L0.mT, 1)

            def turn_h(k, j):
                q = (k.par * PAIRS + j) % 2
                pe.wait_ge(L0.relu, k.count(2 * B, 4 * j + 4))
                wait(pe, L0.hT_sb, k.count(PAIRS, j - 1))
                out4 = ps_hT[q][:, :].rearrange("c (t s n) -> c t s n", t=2, s=2)
                for t in range(2):
                    nc.tensor.transpose(out4[:, t, 0, 0:NODES], hn[:, q, t, :], ident[0:NODES, 0:NODES])
                    last = nc.tensor.transpose(out4[:, t, 1, :], hs[:, q, t, :], ident[:])
                last.then_inc(L0.hT, 1)

            def project(k, j):
                q = (k.par * PAIRS + j) % 2
                pe.wait_ge(L0.hT_sb, k.count(PAIRS, j + 1))
                for t in range(2):
                    n = 2 * j + t
                    wait(pe, L0.qkv_sb, k.count(B, n - 1))
                    nc.tensor.matmul(ps_qkv[n % 2][:, 0:D], hT[:, q, t, 0, :], w0[:, 0, :], start=True, stop=False)
                    nc.tensor.matmul(ps_qkv[n % 2][:, 0:D], ones_b[:], bsplit[:, 0:D], start=False, stop=True)
                    kv = ps_qkv[n % 2][:, D:3 * D]
                    nc.tensor.matmul(kv, hT[:, q, t, 1, :], w0[:, 1:3, :].rearrange("c j n -> c (j n)"),
                                     start=True, stop=False)
                    nc.tensor.matmul(kv, ones_b[:], bsplit[:, D:3 * D], start=False, stop=True
                                     ).then_inc(L0.qkv, 1)

            def skip_and_qe(k, j):
                p, q = k.par, (k.par * PAIRS + j) % 2
                pe.wait_ge(L0.qkv_sb, k.count(B, 2 * j + 2))
                if j == 0:
                    pe.wait_ge(L0.mT_sb, k.count(3, 3))
                    wait(pe, L0.tile, k.plus(-1).count(N_TILE, N_TILE))
                else:
                    pe.wait_ge(L0.tile, k.count(N_TILE, 3 * j - 1))
                for t in range(2):
                    sk = ps_dv[:, t * D:(t + 1) * D]
                    nc.tensor.matmul(sk, hT[:, q, t, 0, :], w0[:, 3, :], start=True, stop=False)
                    nc.tensor.matmul(sk, ones_b[:], bsplit[:, 3 * D:4 * D], start=False, stop=True)
                for t in range(2):
                    last = nc.tensor.matmul(ps_dv[:, (2 + t) * D:(3 + t) * D], memberT[:, 2 * j + t, :],
                                            qkv[0:NODES, p, 2 * j + t, 0:D], start=True, stop=True)
                last.then_inc(L0.dv, 1)

            def turn_alpha(k):
                pe.wait_ge(L0.tile, k.count(N_TILE, N_TILE))
                pe.wait_ge(L0.seg, k.plus(1).count(N_SEG, 1) if exists(k.plus(1)) else
                           k.count(N_SEG, 1))
                if exists(k.plus(3)):
                    pe.wait_ge(L0.idx, k.plus(3).count(N_IDX, N_IDX))
                nc.tensor.transpose(ps_misc[:, 0:WIN], alpha[:, k.par, :], ident[:]).then_inc(L0.aT, 1)

            def turn_max(k):
                pe.wait_ge(L0.mid, k.count(N_MID, 2))
                pe.sem_inc(L0.small_turn, 1)
                nc.tensor.transpose(ps_misc[:, 0:BH], smax[:], ident[0:BH, 0:BH]).then_inc(L0.maxT, 1)

            def aggregate(k, j):
                p = k.par
                pe.wait_ge(L0.mid, k.count(N_MID, 4))
                wait(pe, L0.fin, k.count(N_FIN, 4 * j - 1))
                for t in range(2):
                    last = nc.tensor.matmul(ps_agg[0:NODES, t * (D + 4):(t + 1) * (D + 4)],
                                            member[:, p, 2 * j + t, :], vw[:, p, 2 * j + t, :],
                                            start=True, stop=True)
                last.then_inc(L0.agg, 1)

            def step0(k):
                this, prev = exists(k), exists(k.plus(-1))
                if this:
                    spread_rows(k)
                for j in range(PAIRS):
                    behind, a = pairs_ahead(k, j - 1)
                    if exists(behind) and (this or j == 0):
                        skip_and_qe(behind, a)
                    if this and j == 0:
                        turn_members(k, 0)
                        if exists(k.plus(2)):
                            turn_idx(k.plus(2))
                    ahead, a = pairs_ahead(k, j + 1)
                    if this and exists(ahead):
                        turn_h(ahead, a)
                    if this and j == 0:
                        turn_members(k, 1)
                    if this:
                        project(k, j)
                    if this and j == 0:
                        turn_members(k, 2)
                    if prev:
                        if j == 0:
                            turn_alpha(k.plus(-1))
                        if j == 1:
                            turn_max(k.plus(-1))
                        for n in ((), (), (0,), (1, 2), (3, 4))[j]:
                            aggregate(k.plus(-1), n)

            for n in range(2):
                turn_idx(Batch(n))
            turn_h(Batch(0), 0)
            steps(pe, step0, 0, BATCHES)

            def turn_and_sum(k, t):
                p, q = k.par, (k.par * PAIRS + t // 2) % 2
                pe.wait_ge(L1.relu, k.count(2 * B, 2 * t + 2))
                if t == 0:
                    pe.wait_ge(L1.member, k.count(1, 1))
                    pe.wait_ge(L1.ea[p], k.half(16 * B, 16 * B))
                wait(pe, L1.hT_sb, k.count(B, t - 1))
                ps = ps_t1[t % 2]
                nc.tensor.transpose(ps[:, 0:NODES], hn[:, q, t % 2, :], ident[0:NODES, 0:NODES])
                nc.tensor.matmul(ps[:, NODES:2 * NODES], hs[:, q, t % 2, :], member[:, p, t, :], start=True, stop=True)
                nc.tensor.matmul(ps[:, 2 * NODES:3 * NODES], eaw[:, p, t, :], member[:, p, t, :],
                                 start=True, stop=True).then_inc(L1.agg, 1)

            def project1(k, t):
                j, q = t // 2, (k.par * PAIRS + t // 2) % 2
                pe.wait_ge(L1.hT_sb, k.count(B, t + 1))
                if t % 2 == 0:
                    wait(pe, L1.tile, k.count(3 * PAIRS, 3 * (j - 1)))
                a = ps_self[q][0:NODES, (t % 2) * D:(t % 2 + 1) * D]
                nc.tensor.matmul(a, aggT[:, t % 2, 0, :], w1[:, 0:D], start=True, stop=False)
                nc.tensor.matmul(a, ones_b[:, 0:NODES], bsplit[:, 4 * D:5 * D], start=False, stop=True)
                m = ps_msg[q][0:NODES, (t % 2) * (D + 4):(t % 2 + 1) * (D + 4)]
                nc.tensor.matmul(m, aggT[:, t % 2, 1, :], w1m[:], start=True, stop=False)
                nc.tensor.matmul(m, aggT[:, t % 2, 2, :], weaug[:], start=False, stop=True).then_inc(L1.qkv, 1)

            def step1(k):
                for j in range(PAIRS):
                    ahead, a = pairs_ahead(k, j + 1)
                    for t in range(2):
                        project1(k, 2 * j + t)
                        if exists(ahead):
                            turn_and_sum(ahead, 2 * a + t)

            def long_rows_projected(S):
                def before(i, tile, n):
                    pe.wait_ge(S.act_tile, i * T_ACT[S.n] + 1)
                    nc.tensor.transpose(ps_hT[0][:, 0:NODES], hn[:, 0, 0, :], ident[0:NODES, 0:NODES]
                                        ).then_inc(S.pe_tile, 1)
                    pe.wait_ge(S.act_tile, i * T_ACT[S.n] + 2)
                    rows = hT[:, 0, 0, 0, 0:NODES]
                    if S is S0:
                        targets = ((ps_qkv[0], w0[:, 0, :], 0), (ps_dv, w0[:, 3, :], 3 * D))
                    else:
                        targets = ((ps_self[0], w1[:, 0:D], 4 * D),)
                    for to, w, b in targets:
                        nc.tensor.matmul(to[0:NODES, 0:D], rows, w, start=True, stop=False)
                        last = nc.tensor.matmul(to[0:NODES, 0:D], ones_b[:, 0:NODES], bsplit[:, b:b + D],
                                                start=False, stop=True)
                    last.then_inc(S.pe_tile, 1)
                return before

            def long_chunk0(c, tile, n):
                S, dve_base = S0, n * C_DVE[0] + (STAT_STEPS + 4)
                pe.wait_ge(S.act, n * C_ACT[0] + 1)
                nc.tensor.transpose(ps_hT[0][:, 0:ROWS], hs[0:ROWS, 0, 0, :], ident[0:ROWS, 0:ROWS])
                nc.tensor.transpose(ps_mT[0:NODES, 0:ROWS], member[0:ROWS, 0, 0, :], ident[0:ROWS, 0:ROWS]
                                    ).then_inc(S.pe, 1)
                pe.wait_ge(S.act, n * C_ACT[0] + 2)
                kv = ps_qkv[1][0:ROWS, 0:2 * D]
                nc.tensor.matmul(kv, hT[:, 0, 0, 1, 0:ROWS], w0[:, 1:3, :].rearrange("c j n -> c (j n)"),
                                 start=True, stop=False)
                nc.tensor.matmul(kv, ones_b[:, 0:ROWS], bsplit[:, D:3 * D], start=False, stop=True)
                nc.tensor.matmul(ps_dv[0:ROWS, 0:D], memberT[:, 0, 0:ROWS], qkv[0:NODES, 0, 0, 0:D],
                                 start=True, stop=True).then_inc(S.pe, 1)
                pe.wait_ge(S.dve, dve_base + 3)
                for h in range(HEADS):
                    last = nc.tensor.transpose(ps_agg[0:NODES, h * ROWS:(h + 1) * ROWS], masked[:, h, :],
                                               ident[0:ROWS, 0:ROWS])
                last.then_inc(S.pe, 1)
                pe.wait_ge(S.dve, dve_base + 5)
                nc.tensor.matmul(ps_misc[0:ROWS, 0:HEADS], memberT[:, 0, 0:ROWS], new_max[:], start=True, stop=True
                                 ).then_inc(S.pe, 1)
                pe.wait_ge(S.dve, dve_base + 10)
                nc.tensor.matmul(ps_agg[0:NODES, 0:D + HEADS], member[0:ROWS, 0, 0, :], vw[0:ROWS, 0, 0, :],
                                 start=True, stop=True).then_inc(S.pe, 1)

            def long_chunk1(c, tile, n):
                pe.wait_ge(S1.feat, n * 16)
                pe.wait_ge(S1.act, n * C_ACT[1] + 1)
                ps = ps_t1[1]
                nc.tensor.matmul(ps[:, 0:NODES], hs[0:ROWS, 0, 0, :], member[0:ROWS, 0, 0, :], start=True, stop=True)
                nc.tensor.matmul(ps[:, NODES:2 * NODES], eaw[0:ROWS, 0, 0, :], member[0:ROWS, 0, 0, :],
                                 start=True, stop=True).then_inc(S1.pe, 1)
                pe.wait_ge(S1.act, n * C_ACT[1] + 2)
                m = ps_msg[0][0:NODES, 0:D + HEADS]
                nc.tensor.matmul(m, aggT[:, 0, 1, :], w1m[:], start=True, stop=False)
                nc.tensor.matmul(m, aggT[:, 0, 2, :], weaug[:], start=False, stop=True).then_inc(S1.pe, 1)

            long_tiles(pe, L0, S0, long_rows_projected(S0), long_chunk0, None)
            pe.wait_ge(long_done[0], 1)
            turn_and_sum(Batch(0), 0)
            turn_and_sum(Batch(0), 1)
            steps(pe, step1, 0, BATCHES - 1)
            long_tiles(pe, L1, S1, long_rows_projected(S1), long_chunk1, None)


_ORDER = ["x", "edges", "edge_attr_64", "L0_gnn_Wq", "L0_gnn_bq", "L0_gnn_Wk", "L0_gnn_bk", "L0_gnn_Wv", "L0_gnn_bv",
          "L0_gnn_Wskip", "L0_gnn_bskip", "L1_gnn_W_kernel", "L1_gnn_W_bias", "L1_gnn_We_kernel", "L1_gnn_We_bias"]


def kernel(**inputs):
    import concourse.bacc as bacc
    from concourse.bass_utils import run_bass_kernel_spmd

    arrays = {n: np.ascontiguousarray(v) for n, v in inputs.items()}
    arrays["edges"] = np.stack([arrays.pop("src"), arrays.pop("dst")], axis=1)
    nc = bacc.Bacc("TRN2", target_bir_lowering=False, num_devices=1)
    ins = {f"in_{n}": arrays[n] for n in _ORDER}
    args = [nc.dram_tensor(n, a.shape, mybir.dt.from_np(a.dtype), kind="ExternalInput").ap() for n, a in ins.items()]
    out = nc.dram_tensor("out_rows", (N, D), F32, kind="ExternalOutput").ap()
    build(nc, *args, out)
    r = run_bass_kernel_spmd(nc, [ins], core_ids=[0])
    return r.results[0]["out_rows"]
```

```python
from contextlib import ExitStack

import numpy as np

import concourse.bass as bass
from concourse import mybir
from concourse.alu_op_type import AluOpType as ALU

F32 = mybir.dt.float32
BF16 = mybir.dt.bfloat16
I32 = mybir.dt.int32
ACT = mybir.ActivationFunctionType
AX_X = mybir.AxisListType.X

N, D, E, HEADS, DE = 50000, 128, 50000, 4, 64
CH = D // HEADS
NODES = 100
TILES = N // NODES
WIN = 128
B = 10
BATCHES = TILES // B
PAIRS = B // 2
BH = B * HEADS
FIRST = PAIRS - 1
EPS = 1e-5
BIG = 3.0e38
SCALE = 1.0 / float(np.sqrt(CH))
ROWS = 125
EROWS = E // ROWS
TG = TILES // ROWS

RSQRT_BITS = float(0x5F3759DF)
NEWTON = 3

N_IDX, N_SEG, N_STAT, N_TILE, N_MID, N_FIN = 4, 3, 4 + 3 * NEWTON, 3 * PAIRS, 4, 3 * PAIRS
N_OUT = 3 * PAIRS


def fin_count(j, n):
    return n + 1 if j == 0 else 3 + 6 * ((j - 1) // 2) + 2 * n + (j - 1) % 2 + 1


STAT_STEPS = N_STAT + 1
T_DVE = (STAT_STEPS + 8, STAT_STEPS + 6)
T_ACT = (3, 2)
T_PE = (2, 2)
C_DVE = (STAT_STEPS + 16, STAT_STEPS + 4)
C_ACT = (4, 2)
C_PE = (5, 2)
NEVER = 2.0 * TILES


class Batch:

    def __init__(self, off, i=None):
        self.off, self.i = off, i

    def plus(self, n):
        return Batch(self.off + n, self.i)

    @property
    def par(self):
        return self.off % 2

    @property
    def known(self):
        return self.i is None

    def count(self, per, n):
        return self.off * per + n if self.known else self.i * (2 * per) + (self.off * per + n)

    def half(self, per, n):
        return (self.off // 2) * per + n if self.known else self.i * per + ((self.off // 2) * per + n)


def wait(eng, sem, value):
    if isinstance(value, int) and value <= 0:
        return
    eng.wait_ge(sem, value)


def pairs_ahead(k, j):
    return k.plus(j // PAIRS), j % PAIRS


def exists(k):
    return not k.known or 0 <= k.off < BATCHES


def steps(eng, body, first, last):
    inner = first + 4
    rounds = (BATCHES - 5 - inner) // 2
    for n in range(first, inner):
        body(Batch(n))
    with eng.Fori(0, rounds) as i:
        for n in (inner, inner + 1):
            body(Batch(n, i))
    for n in range(inner + 2 * rounds, last + 1):
        body(Batch(n))


def build(nc, x, edges, ea, Wq, bq, Wk, bk, Wv, bv, Ws, bs, W1, b1, We, be, out):
    x1 = nc.dram_tensor("x1_rows", (N, D), F32, kind="Internal").ap()
    starts_dram = nc.dram_tensor("window_starts", (2 * TG, ROWS), I32, kind="Internal").ap()

    with ExitStack() as ctx:
        def sb(name, shape, dt=F32):
            return ctx.enter_context(nc.sbuf_tensor("sb_" + name, shape, dt))

        def bank(name):
            return ctx.enter_context(nc.psum_tensor("ps_" + name, [128, 512], F32))

        def sem(name):
            return ctx.enter_context(nc.semaphore(name))

        ident = sb("ident", [128, 128])
        iota = sb("iota", [128, NODES])
        n0tab = sb("n0tab", [B, BATCHES])
        rep = sb("rep", [B, BH])
        ones = sb("ones", [128, 128])
        ones_b = sb("ones_b", [128, 128], BF16)
        w0 = sb("w0", [128, 4, D])
        w1 = sb("w1", [128, 2 * D])
        w1m = sb("w1m", [128, D + 4])
        weaug = sb("weaug", [128, D + 4])
        brow = sb("brow", [1, 6, D])
        berow = sb("berow", [1, D])
        bmsg = sb("bmsg", [1, D + 4])
        bres = sb("bres", [1, 2, 5 * D])
        bpart = sb("bpart", [1, 3, 5 * D], BF16)
        bsplit = sb("bsplit", [128, 5 * D], BF16)

        heads_i = sb("heads_i", [1, EROWS], I32)
        heads_f = sb("heads_f", [1, EROWS])
        thr = sb("thr", [ROWS, TG])
        cmp1 = sb("cmp1", [ROWS, TG, EROWS])
        cnt1 = sb("cnt1", [ROWS, TG])
        row_f = sb("row_f", [ROWS, TG])
        row_i = sb("row_i", [ROWS, TG], I32)
        row_e = sb("row_e", [ROWS, TG, 2 * ROWS], I32)
        cmp2 = sb("cmp2", [ROWS, TG, ROWS])
        cnt2 = sb("cnt2", [ROWS, TG])
        lo_f = sb("lo_f", [ROWS, TG])
        st_f = sb("st_f", [ROWS, 2 * TG])
        st_i = sb("st_i", [2 * TG, ROWS], I32)
        starts = sb("starts", [1, 2 * TILES + 1], I32)

        all_e = sb("all_e", [ROWS, 2 * EROWS], I32)
        next_e = sb("next_e", [ROWS, 1], I32)
        falls = sb("falls", [ROWS, EROWS])
        falls_any = sb("falls_any", [ROWS, 1])
        unsorted = sb("unsorted", [1, 3])
        tile_no = sb("tile_no", [1, TILES])
        zeros = sb("zeros", [1, TILES])
        cmp1_row = cmp1[0:1, :, :].rearrange("o g r -> o (g r)")
        run_len, is_long, later = (cmp1_row[:, n * TILES:(n + 1) * TILES] for n in range(3))
        later_min = sb("later_min", [1, TILES])
        chunk_lo = sb("chunk_lo", [1, TILES])
        chunk_hi = sb("chunk_hi", [1, TILES])
        long_count_f = sb("long_count_f", [1, 1])
        long_count = sb("long_count", [1, 1], I32)
        next_long = sb("next_long", [1, TILES], I32)
        first_chunk = sb("first_chunk", [1, TILES], I32)
        end_chunk = sb("end_chunk", [1, TILES], I32)

        n0all = sb("n0all", [128, TILES])
        chunk_e = sb("chunk_e", [ROWS, 2], I32)
        chunk_d = sb("chunk_d", [ROWS, 1])
        outside = sb("outside", [ROWS, NODES])
        masked = sb("masked", [ROWS, HEADS, NODES])
        acc = sb("acc", [NODES, D + HEADS])
        run_max = sb("run_max", [NODES, HEADS])
        chunk_max = sb("chunk_max", [NODES, HEADS])
        new_max = sb("new_max", [NODES, HEADS])
        max_step = sb("max_step", [NODES, HEADS])
        rescale = sb("rescale", [NODES, HEADS])

        rows_i = sb("rows_i", [B, 2, 2 * WIN], I32)
        rows_f = sb("rows_f", [B, 2, 2, WIN])
        src_idx = sb("src_idx", [128, 2, B], I32)
        src_all = sb("src_all", [128, TILES], I32)
        drel_all = sb("drel_all", [128, TILES])
        drep = sb("drep", [BH, WIN])
        dne = sb("dne", [BH, WIN - 1])
        segm = sb("segm", [BH, 2, WIN + 1])
        member = sb("member", [128, 2, B, NODES])
        memberT = sb("memberT", [NODES, 2, B, WIN])
        xn = sb("xn", [NODES, 2, B, D])
        xs = sb("xs", [128, 2, B, D])
        st = sb("st", [128, 2, 2 * B, 6])
        ssum = sb("ssum", [128, 2 * B])
        sdif = sb("sdif", [128, 2 * B])
        svar = sb("svar", [128, 2 * B])
        sd2 = sb("sd2", [128, 2 * B])
        sv2 = sb("sv2", [128, 2 * B])
        var = sb("var", [128, 2 * B])
        guess = sb("guess", [128, 2, 2 * B], I32)
        nwt = sb("nwt", [128, 2, 2 * B])
        rstd = sb("rstd", [128, 2, 2 * B])
        shift = sb("shift", [128, 2, 2 * B])
        hn = sb("hn", [NODES, 2, 2, D])
        hs = sb("hs", [128, 2, 2, D])
        hT = sb("hT", [128, PAIRS, 2, 2, 128])
        qkv = sb("qkv", [128, 2, B, 3 * D])
        prod = sb("prod", [128, 2, D])
        alpha = sb("alpha", [128, 2, 128])
        fmax = sb("fmax", [BH, WIN])
        smax = sb("smax", [BH, WIN])
        dl = sb("dl", [128, BH])
        vw = sb("vw", [128, 2, B, D + 4])
        xsk = sb("xsk", [NODES, 2, B, D])
        den = sb("den", [NODES, 2, 2, HEADS])
        rden = sb("rden", [NODES, 2, 2, HEADS])
        yself = sb("yself", [NODES, 2, D])
        xo = sb("xo", [NODES, 2, B, D])
        eaw = sb("eaw", [128, 2, B, 128])
        aggT = sb("aggT", [128, 2, 3, NODES])
        deg = sb("deg", [NODES, 2, 1])

        banks = [bank(f"b{n}") for n in range(8)]
        ps_hT, ps_qkv = banks[0:2], banks[2:4]
        ps_dv, ps_misc, ps_agg, ps_mT = banks[4], banks[5], banks[6], banks[7]
        ps_pair = [ps_agg, ps_mT]
        ps_t1, ps_self, ps_msg = banks[0:2], banks[2:4], [banks[4], banks[6]]

        const_load = sem("const_load")
        const_made = sem("const_made")
        bias_step = sem("bias_step")
        bias_placed = sem("bias_placed")
        search = sem("search")
        heads_load = sem("heads_load")
        heads_spread = sem("heads_spread")
        rows_gather = sem("rows_gather")
        starts_turned = sem("starts_turned")
        starts_out = sem("starts_out")
        starts_in = sem("starts_in")
        zeroed = sem("zeroed")
        all_edges_load = sem("all_edges_load")
        list_step = sem("list_step")
        falls_summed = sem("falls_summed")
        long_done = [sem("L0_long_done"), sem("L1_long_done")]

        class Layer:

            def __init__(self, n):
                def s(name):
                    return sem(f"L{n}_{name}")
                self.win = [s("win_loaded0"), s("win_loaded1")]
                self.xn = [[s("nodes_loaded0"), s("nodes_loaded1")], [s("last_nodes_loaded0"), s("last_nodes_loaded1")]]
                self.ea = [s("edge_feat_loaded0"), s("edge_feat_loaded1")]
                self.gat = [s("gathered0"), s("gathered1")]
                self.stored = [s("stored0"), s("stored1")]
                self.idx = s("idx_step")
                self.turned_idx = s("idx_turned")
                self.pair_free = s("pair_free")
                self.cols = s("gather_cols_ready")
                self.small_turn = s("small_turn_starts")
                self.member = s("member_built")
                self.bn = s("bn_stats_done")
                self.stat = s("stat_step")
                self.seg = s("segment_step")
                self.spread = s("rows_spread")
                self.shift = s("shift_ready")
                self.relu = s("relu_done")
                self.hT = s("h_turned")
                self.hT_sb = s("h_turned_copied")
                self.mT = s("member_turned")
                self.mT_sb = s("member_turned_copied")
                self.qkv = s("qkv_ready")
                self.qkv_sb = s("qkv_copied")
                self.dv = s("skip_and_qe_ready")
                self.tile = s("tile_step")
                self.aT = s("alpha_turned")
                self.maxT = s("max_turned")
                self.mid = s("mid_step")
                self.exp = s("exp_done")
                self.agg = s("agg_ready")
                self.fin = s("fin_step")
                self.added = s("skip_added")

        class LongTiles:

            def __init__(self, n):
                def s(name):
                    return sem(f"L{n}_long_{name}")
                self.n = n
                self.rows = s("rows_loaded")
                self.edges = s("edges_loaded")
                self.feat = s("features_loaded")
                self.gathered = s("gathered")
                self.stored = s("stored")
                self.go = s("waits_over")
                self.dve_tile, self.act_tile, self.pe_tile = s("dve_tile"), s("act_tile"), s("pe_tile")
                self.dve, self.act, self.pe = s("dve_chunk"), s("act_chunk"), s("pe_chunk")
                self.first = {
                    "SP": [],
                    "Pool": [],
                    "DVE": [(self.dve_tile, T_DVE[n]), (self.dve, C_DVE[n])],
                    "Activation": [(self.act_tile, T_ACT[n]), (self.act, C_ACT[n])],
                    "PE": [(self.pe_tile, T_PE[n]), (self.pe, C_PE[n])],
                }

        L0, L1 = Layer(0), Layer(1)
        S0, S1 = LongTiles(0), LongTiles(1)
        block = ctx.enter_context(nc.Block())

        dst_rows = edges.rearrange("(r c) two -> r (c two)", c=ROWS)

        def long_tiles(eng, L, S, before, chunk, after):
            for p in range(2):
                eng.wait_ge(L.stored[p], 16 * (BATCHES // 2))
            eng.wait_ge(list_step, 13)
            count = eng.value_load(long_count[0:1, 0:1], min_val=0, max_val=TILES)
            cursor = eng.alloc_register(f"L{S.n}_cursor_{eng.engine.name}")
            chunks = eng.alloc_register(f"L{S.n}_chunks_{eng.engine.name}")
            eng.reg_mov(cursor, 0)
            eng.reg_mov(chunks, 1)
            for primed, by in S.first[eng.engine.name]:
                eng.sem_inc(primed, by)
            with eng.If(count > 0):
                with eng.Fori(1, count + 1) as i:
                    tile = eng.value_load(next_long[0:1, bass.ds(eng.snap(cursor), 1)], min_val=0, max_val=TILES - 1)
                    first = eng.value_load(first_chunk[0:1, bass.ds(tile, 1)], min_val=0, max_val=EROWS - 1)
                    end = eng.value_load(end_chunk[0:1, bass.ds(tile, 1)], min_val=1, max_val=EROWS)
                    if before:
                        before(i, tile, eng.snap(chunks))
                    with eng.Fori(first, end) as c:
                        if chunk:
                            chunk(c, tile, eng.snap(chunks))
                        eng.reg_add(chunks, chunks, 1)
                    if after:
                        after(i, tile, eng.snap(chunks))
                    eng.reg_mov(cursor, tile + 1)

        @block.sync
        def _(sp):
            for j, w in enumerate((Wq, Wk, Wv, Ws)):
                sp.dma_start(w0[:, j, :], w).then_inc(const_load, 16)
            sp.dma_start(w1[:], W1).then_inc(const_load, 16)
            sp.wait_ge(zeroed, 1)
            sp.dma_start(weaug[0:DE, 0:D], We).then_inc(const_load, 16)
            for j, b in enumerate((bq, bk, bv, bs)):
                sp.dma_start(brow[:, j, :], b.rearrange("(o n) -> o n", o=1)).then_inc(const_load, 16)
            sp.dma_start(brow[:, 4:6, :].rearrange("o j n -> o (j n)"),
                         b1.rearrange("(o n) -> o n", o=1)).then_inc(const_load, 16)
            sp.dma_start(berow[:], be.rearrange("(o n) -> o n", o=1)).then_inc(const_load, 16)
            with nc.allow_non_contiguous_dma(reason="400 words, once"):
                sp.dma_start(heads_i[:], edges.rearrange("(r c) two -> r c two", c=ROWS)[:, 0, 1:2]
                             .rearrange("r o -> o r")).then_inc(heads_load, 16)
            sp.dma_start(all_e[:], edges.rearrange("(r c) two -> r (c two)", c=EROWS)).then_inc(all_edges_load, 16)
            sp.wait_ge(list_step, 1)
            with nc.allow_non_contiguous_dma(reason="a word a partition, once"):
                sp.dma_start(next_e[0:ROWS - 1, :], edges.rearrange("(r c) two -> r c two", c=EROWS)[1:ROWS, 0, 1:2]
                             ).then_inc(all_edges_load, 16)
            sp.wait_ge(search, 9)
            sp.dma_start(starts_dram, st_i[:]).then_inc(starts_out, 16)
            sp.wait_ge(starts_out, 16)
            sp.dma_start(starts[0:1, 0:2 * TILES], starts_dram.rearrange("(o g) r -> o (g r)", o=1)
                         ).then_inc(starts_in, 16)
            sp.wait_ge(bias_step, 7)
            sp.dma_start(bsplit[0:3, :], bpart[0:1, :, :]).then_inc(bias_placed, 16)
            sp.dma_start(weaug[DE:DE + 1, :], bmsg[:]).then_inc(bias_placed, 16)
            sp.wait_ge(starts_in, 16)

            def batch_starts(k):
                _, found = nc.values_load_multi_w_load_instructions(
                    starts[0:1, bass.ds(k.count(B, 0), B)], engines=(sp.engine,), min_val=0, max_val=E - WIN,
                    skip_runtime_bounds_check_because="counts of edges, held to E - WIN where they were made")
                return found

            def windows(k):
                p = k.par
                wait(sp, L0.idx, k.plus(-2).count(N_IDX, 2))
                sp.wait_ge(starts_in, 16)
                for t, start in enumerate(batch_starts(k)):
                    sp.dma_start(rows_i[t:t + 1, p, :],
                                 edges[bass.ds(start, WIN), :].rearrange("(o e) two -> o (e two)", o=1)
                                 ).then_inc(L0.win[p], 16)

            def features(k):
                p = k.par
                wait(sp, L1.agg, k.plus(-2).count(B, B))
                sp.wait_ge(starts_in, 16)
                for t, start in enumerate(batch_starts(k)):
                    sp.dma_start(eaw[:, p, t, 0:DE], ea[bass.ds(start, WIN), :]).then_inc(L1.ea[p], 16)

            def nodes(L, k, table, part):
                p = k.par
                first, last = ((0, 2 * FIRST), (2 * FIRST, B))[part]
                wait(sp, L.tile, k.plus(-2).count(N_TILE, 3 * last // 2))
                rows = table[bass.ds(k.count(B * NODES, first * NODES), (last - first) * NODES), :]
                sp.dma_start(xn[:, p, first:last, :], rows.rearrange("(t n) d -> n t d", n=NODES)
                             ).then_inc(L.xn[part][p], 16)

            def store(L, k, table, done_sem, per):
                p = k.par
                sp.wait_ge(done_sem, k.count(per, per))
                rows = table[bass.ds(k.count(B * NODES, 0), B * NODES), :]
                sp.dma_start(rows.rearrange("(t n) d -> n t d", n=NODES), xo[:, p, :, :]).then_inc(L.stored[p], 16)

            def step(L, table, to, done, per, k):
                if exists(k.plus(1)):
                    nodes(L, k.plus(1), table, 1)
                if L is L1 and exists(k.plus(-1)):
                    store(L, k.plus(-1), to, done, per)
                if L is L1 and exists(k.plus(1)):
                    features(k.plus(1))
                if L is L0 and exists(k.plus(-2)):
                    store(L, k.plus(-2), to, done, per)
                if L is L0 and exists(k.plus(4)):
                    windows(k.plus(4))
                if exists(k.plus(2)):
                    nodes(L, k.plus(2), table, 0)

            windows(Batch(0))
            for part in (0, 1):
                nodes(L0, Batch(0), x, part)
            windows(Batch(1))
            nodes(L0, Batch(1), x, 0)
            windows(Batch(2))
            windows(Batch(3))
            steps(sp, lambda k: step(L0, x, x1, L0.added, 1, k), 0, BATCHES + 1)

            def long_rows(L, S, table):
                def before(i, tile, n):
                    sp.wait_ge(S.dve_tile, i * T_DVE[S.n])
                    sp.sem_inc(S.go, 1)
                    sp.dma_start(xn[:, 0, 0, :], table[bass.ds(tile * NODES, NODES), :]).then_inc(S.rows, 16)
                return before

            def long_edges(S):
                def chunk(c, tile, n):
                    sp.wait_ge(S.dve, n * C_DVE[S.n])
                    sp.sem_inc(S.go, 1)
                    sp.dma_start(chunk_e[:], edges[bass.ds(c * ROWS, ROWS), :]).then_inc(S.edges, 16)
                    if S is S1:
                        sp.dma_start(eaw[0:ROWS, 0, 0, 0:DE], ea[bass.ds(c * ROWS, ROWS), :]).then_inc(S.feat, 16)
                return chunk

            def long_store(S, to):
                def after(i, tile, n):
                    sp.wait_ge(S.dve_tile, i * T_DVE[S.n] + T_DVE[S.n])
                    sp.sem_inc(S.go, 1)
                    sp.dma_start(to[bass.ds(tile * NODES, NODES), :], xo[:, 0, 0, :]).then_inc(S.stored, 16)
                    sp.wait_ge(S.stored, i * 16)
                    sp.sem_inc(S.go, 1)
                return after

            long_tiles(sp, L0, S0, long_rows(L0, S0, x), long_edges(S0), long_store(S0, x1))
            sp.sem_inc(long_done[0], 1)
            sp.wait_ge(long_done[0], 1)
            for part in (0, 1):
                nodes(L1, Batch(0), x1, part)
            nodes(L1, Batch(1), x1, 0)
            features(Batch(0))
            steps(sp, lambda k: step(L1, x1, out, L1.tile, N_OUT, k), 0, BATCHES)
            long_tiles(sp, L1, S1, long_rows(L1, S1, x1), long_edges(S1), long_store(S1, out))

        @block.gpsimd
        def _(pool):
            pool.memset(ones[:], 1.0).then_inc(const_made, 1)
            pool.memset(ident[:], 0.0).then_inc(const_made, 1)
            pool.memset(rep[:], 0.0).then_inc(const_made, 1)
            pool.iota(iota[:], pattern=[[1, NODES]], base=0, channel_multiplier=0,
                      allow_small_or_imprecise_dtypes=True).then_inc(const_made, 1)
            pool.iota(n0tab[:], pattern=[[B * NODES, BATCHES]], base=0, channel_multiplier=NODES,
                      allow_small_or_imprecise_dtypes=True).then_inc(const_made, 1)
            pool.iota(thr[:], pattern=[[ROWS * NODES, TG]], base=0, channel_multiplier=NODES,
                      allow_small_or_imprecise_dtypes=True).then_inc(const_made, 1)
            pool.iota(tile_no[:], pattern=[[1, TILES]], base=0, channel_multiplier=0,
                      allow_small_or_imprecise_dtypes=True).then_inc(const_made, 1)
            pool.iota(n0all[:], pattern=[[NODES, TILES]], base=0, channel_multiplier=0,
                      allow_small_or_imprecise_dtypes=True).then_inc(const_made, 1)
            pool.wait_ge(const_made, 8)
            pool.affine_select(out=ident[:], in_=ident[:], compare_op=ALU.not_equal, fill=1.0, base=0,
                               pattern=[[-1, 128]], channel_multiplier=1).then_inc(const_made, 1)
            pool.affine_select(out=rep[:].rearrange("p (t h) -> p t h", h=HEADS),
                               in_=rep[:].rearrange("p (t h) -> p t h", h=HEADS),
                               compare_op=ALU.not_equal, fill=1.0, base=0,
                               pattern=[[-1, B], [0, HEADS]], channel_multiplier=1).then_inc(const_made, 1)
            pool.wait_ge(search, 4)
            for g in range(TG):
                pool.indirect_dma_start(out=row_e[:, g, :], out_offset=None, in_=dst_rows,
                                        in_offset=bass.IndirectOffsetOnAxis(ap=row_i[:, g:g + 1], axis=0)
                                        ).then_inc(rows_gather, 16)

            def gathers(L, k, table):
                p = k.par
                pool.wait_ge(L.cols, k.count(1, 1))
                for t in range(B):
                    if t % 2 == 0:
                        wait(pool, L.relu, k.plus(-2).count(2 * B, 2 * t + 4))
                        pool.sem_inc(L.pair_free, 1)
                    pool.indirect_dma_start(out=xs[:, p, t, :], out_offset=None, in_=table,
                                            in_offset=bass.IndirectOffsetOnAxis(ap=src_idx[:, p, t:t + 1], axis=0)
                                            ).then_inc(L.gat[p], 16)
                    if L is L0 and t == 3 and exists(k.plus(-4)):
                        add_skip(k.plus(-4))

            def add_skip(k):
                p = k.par
                pool.wait_ge(L0.fin, k.count(N_FIN, N_FIN))
                pool.wait_ge(L0.tile, k.count(N_TILE, N_TILE))
                pool.tensor_tensor(xo[:, p, :, :], xo[:, p, :, :], xsk[:, p, :, :], ALU.add).then_inc(L0.added, 1)

            def long_gather(S, table):
                def chunk(c, tile, n):
                    pool.wait_ge(S.edges, n * 16)
                    pool.wait_ge(S.act, n * C_ACT[S.n])
                    pool.sem_inc(S.go, 1)
                    pool.indirect_dma_start(out=xs[0:ROWS, 0, 0, :], out_offset=None, in_=table,
                                            in_offset=bass.IndirectOffsetOnAxis(ap=chunk_e[:, 0:1], axis=0)
                                            ).then_inc(S.gathered, 16)
                return chunk

            steps(pool, lambda k: gathers(L0, k, x), 0, BATCHES - 1)
            for n in range(BATCHES - 4, BATCHES):
                add_skip(Batch(n))
            long_tiles(pool, L0, S0, None, long_gather(S0, x), None)
            pool.wait_ge(long_done[0], 1)
            steps(pool, lambda k: gathers(L1, k, x1), 0, BATCHES - 1)
            long_tiles(pool, L1, S1, None, long_gather(S1, x1), None)

        @block.vector
        def _(dve):
            dve.memset(next_e[:], E).then_inc(list_step, 1)
            dve.memset(weaug[:], 0.0).then_inc(zeroed, 1)
            dve.memset(bsplit[:], 0.0).then_inc(zeroed, 1)
            dve.memset(ones_b[:], 1.0).then_inc(zeroed, 1)
            dve.memset(w1m[:], 0.0).then_inc(zeroed, 1)
            dve.memset(bmsg[:], 0.0).then_inc(zeroed, 1)
            dve.memset(st[:], 0.0).then_inc(zeroed, 1)
            dve.memset(hT[:], 0.0).then_inc(zeroed, 1)
            dve.memset(alpha[:], 0.0).then_inc(zeroed, 1)
            dve.memset(segm[:, :, 0:WIN + 1:WIN], -BIG).then_inc(zeroed, 1)
            dve.memset(eaw[:], 0.0).then_inc(zeroed, 1)
            dve.wait_ge(zeroed, 10)
            dve.memset(eaw[:, :, :, DE:DE + 1], 1.0).then_inc(zeroed, 1)

            dve.wait_ge(heads_load, 16)
            dve.tensor_copy(heads_f[:], heads_i[:]).then_inc(search, 1)
            dve.wait_ge(heads_spread, 1)
            dve.wait_ge(const_made, 10)
            for g in range(TG):
                ins = dve.tensor_scalar(cmp1[:, g, :], ps_misc[0:ROWS, 0:EROWS], thr[:, g:g + 1], None, ALU.is_lt)
            ins.then_inc(search, 1)
            dve.wait_ge(search, 2)
            dve.tensor_reduce(cnt1[:], cmp1[:], AX_X, ALU.add).then_inc(search, 1)
            dve.wait_ge(search, 3)
            dve.tensor_scalar(row_f[:], cnt1[:], -1.0, 0.0, ALU.add, ALU.max)
            dve.tensor_scalar(row_i[:], cnt1[:], -1.0, 0.0, ALU.add, ALU.max).then_inc(search, 1)
            dve.wait_ge(rows_gather, 16 * TG)
            for g in range(TG):
                ins = dve.tensor_scalar(cmp2[:, g, :], row_e[:, g, 1::2], thr[:, g:g + 1], None, ALU.is_lt)
            ins.then_inc(search, 1)
            dve.wait_ge(search, 5)
            dve.tensor_reduce(cnt2[:], cmp2[:], AX_X, ALU.add).then_inc(search, 1)
            dve.wait_ge(search, 6)
            dve.scalar_tensor_tensor(lo_f[:], row_f[:], float(ROWS), cnt2[:], ALU.mult, ALU.add).then_inc(search, 1)
            dve.wait_ge(search, 7)
            dve.tensor_scalar(st_f[:, 0:TG], lo_f[:], float(E - WIN), None, ALU.min)
            dve.tensor_copy(st_f[:, TG:2 * TG], lo_f[:]).then_inc(search, 1)
            dve.wait_ge(starts_turned, 1)
            dve.tensor_copy(st_i[:], ps_misc[0:2 * TG, 0:ROWS]).then_inc(search, 1)

            dve.wait_ge(all_edges_load, 32)
            dve.tensor_tensor(falls[:, 0:EROWS - 1], all_e[:, 3::2], all_e[:, 1:2 * EROWS - 1:2], ALU.is_lt)
            dve.tensor_tensor(falls[:, EROWS - 1:EROWS], next_e[:], all_e[:, 2 * EROWS - 1:2 * EROWS], ALU.is_lt
                              ).then_inc(list_step, 1)
            dve.wait_ge(list_step, 2)
            dve.tensor_reduce(falls_any[:], falls[:], AX_X, ALU.max).then_inc(list_step, 1)
            dve.memset(zeros[:], 0.0)
            dve.memset(starts[0:1, 2 * TILES:2 * TILES + 1], E)

            dve.wait_ge(const_load, 16 * 12)
            flat = brow[:].rearrange("o j n -> o (j n)")[:, 0:5 * D]
            dve.tensor_copy(bpart[:, 0, :], flat).then_inc(bias_step, 1)
            dve.wait_ge(bias_step, 1)
            dve.tensor_tensor(bres[:, 0, :], flat, bpart[:, 0, :], ALU.subtract).then_inc(bias_step, 1)
            dve.wait_ge(bias_step, 2)
            dve.tensor_copy(bpart[:, 1, :], bres[:, 0, :]).then_inc(bias_step, 1)
            dve.wait_ge(bias_step, 3)
            dve.tensor_tensor(bres[:, 1, :], bres[:, 0, :], bpart[:, 1, :], ALU.subtract).then_inc(bias_step, 1)
            dve.wait_ge(bias_step, 4)
            dve.tensor_copy(bpart[:, 2, :], bres[:, 1, :]).then_inc(bias_step, 1)
            dve.tensor_tensor(bmsg[:, 0:D], brow[:, 5, :], berow[:], ALU.add).then_inc(bias_step, 1)
            dve.memset(bmsg[:, D:D + 1], 1.0).then_inc(bias_step, 1)
            dve.tensor_copy(w1m[:, 0:D], w1[:, D:2 * D]).then_inc(bias_step, 1)

            dve.wait_ge(falls_summed, 1)
            dve.tensor_scalar(unsorted[:, 0:1], ps_mT[0:1, 0:1], 1.0, None, ALU.min).then_inc(list_step, 1)

            def list_long_tiles():
                lo = starts[0:1, TILES:2 * TILES]
                hi = starts[0:1, TILES + 1:2 * TILES + 1]
                dve.wait_ge(starts_in, 16)
                dve.tensor_tensor(run_len, hi, starts[0:1, 0:TILES], ALU.subtract)
                dve.tensor_scalar(chunk_lo[:], lo, 1.0 / ROWS, -1.0, ALU.mult, ALU.add)
                dve.tensor_scalar(chunk_hi[:], hi, 1.0 / ROWS, 2.0, ALU.mult, ALU.add).then_inc(list_step, 1)
                dve.wait_ge(list_step, 5)
                dve.tensor_scalar(unsorted[:, 1:2], unsorted[:, 0:1], -1.0, 1.0, ALU.mult, ALU.add)
                dve.tensor_scalar(unsorted[:, 2:3], unsorted[:, 0:1], float(EROWS), None, ALU.mult)
                dve.tensor_scalar(is_long, run_len, float(WIN), unsorted[:, 0:1], ALU.is_gt, ALU.max
                                  ).then_inc(list_step, 1)
                dve.wait_ge(list_step, 6)
                dve.tensor_scalar(first_chunk[:], chunk_lo[:], 0.0, unsorted[:, 1:2], ALU.max, ALU.mult)
                dve.tensor_scalar(end_chunk[:], chunk_hi[:], unsorted[:, 2:3], float(EROWS), ALU.max, ALU.min
                                  ).then_inc(list_step, 1)
                dve.tensor_reduce(long_count_f[:], is_long, AX_X, ALU.add).then_inc(list_step, 1)
                dve.tensor_scalar(later, is_long, -NEVER, NEVER, ALU.mult, ALU.add).then_inc(list_step, 1)
                dve.wait_ge(list_step, 9)
                dve.tensor_copy(long_count[:], long_count_f[:]).then_inc(list_step, 1)
                dve.tensor_tensor(later, later, tile_no[:], ALU.add).then_inc(list_step, 1)
                dve.wait_ge(list_step, 11)
                dve.tensor_tensor_scan(later_min[:, ::-1], zeros[:, ::-1], later[:, ::-1], 2 * NEVER,
                                       ALU.add, ALU.min).then_inc(list_step, 1)
                dve.wait_ge(list_step, 12)
                dve.tensor_scalar(next_long[:], later_min[:], float(TILES - 1), None, ALU.min).then_inc(list_step, 1)

            def idx_rows(k):
                p = k.par
                dve.wait_ge(L0.win[p], k.half(16 * B, 16 * B))
                wait(dve, L0.turned_idx, k.plus(-2).count(1, 1))
                wait(dve, L0.spread, k.plus(-2).count(1, 1))
                pairs = rows_i[:, p, :].rearrange("b (e two) -> b e two", two=2)
                dve.tensor_copy(rows_f[:, p, 0, :], pairs[:, :, 0]).then_inc(L0.idx, 1)
                dve.tensor_scalar(rows_f[:, p, 1, :], pairs[:, :, 1], n0tab[:, bass.ds(k.count(1, 0), 1)], None,
                                  ALU.subtract).then_inc(L0.idx, 1)

            def idx_cols(k):
                dve.wait_ge(L0.turned_idx, k.count(1, 1))
                cols = bass.ds(k.count(B, 0), B)
                dve.tensor_copy(src_all[:, cols], ps_misc[:, 0:B]).then_inc(L0.idx, 1)
                dve.tensor_copy(drel_all[:, cols], ps_misc[:, B:2 * B]).then_inc(L0.idx, 1)

            def gather_cols(L, k):
                dve.wait_ge(L0.idx, k.count(N_IDX, 3))
                wait(dve, L.gat[k.par], k.half(16 * B, 0))
                dve.tensor_scalar(src_idx[:, k.par, :], src_all[:, bass.ds(k.count(B, 0), B)], 0, None, ALU.add
                                  ).then_inc(L.cols, 1)

            def segment_mask(k):
                p = k.par
                dve.wait_ge(L0.spread, k.count(1, 1))
                wait(dve, L0.seg, k.plus(-1).count(N_SEG, N_SEG))
                dve.tensor_copy(drep[:], ps_misc[0:BH, 0:WIN]).then_inc(L0.seg, 1)
                dve.wait_ge(L0.seg, k.count(N_SEG, 1))
                dve.tensor_tensor(dne[:], drep[:, 1:WIN], drep[:, 0:WIN - 1], ALU.not_equal).then_inc(L0.seg, 1)
                dve.wait_ge(L0.seg, k.count(N_SEG, 2))
                dve.tensor_scalar(segm[:, p, 1:WIN], dne[:], -BIG, None, ALU.mult).then_inc(L0.seg, 1)

            def members(L, k, first, last, used):
                p, tiles = k.par, last - first
                dve.wait_ge(L0.idx, k.count(N_IDX, 4))
                wait(dve, L.agg, used)
                dve.tensor_tensor(member[:, p, first:last, :],
                                  drel_all[:, bass.ds(k.count(B, first), tiles)].unsqueeze(2)
                                  .to_broadcast([128, tiles, NODES]),
                                  iota[:].unsqueeze(1).to_broadcast([128, tiles, NODES]), ALU.is_equal
                                  ).then_inc(L.member, 1)

            def source_stats(L, k, first=0, last=B):
                p = k.par
                if first == 0:
                    dve.wait_ge(L.gat[p], k.half(16 * B, 16 * B))
                    wait(dve, L.stat, k.plus(-2).count(N_STAT, 1))
                for t in range(first, last):
                    ins = dve.bn_stats(st[:, p, B + t, :], xs[:, p, t, :])
                if last == B:
                    ins.then_inc(L.bn, 1)

            def node_stats(L, k, part):
                p = k.par
                first, last = ((0, 2 * FIRST), (2 * FIRST, B))[part]
                dve.wait_ge(L.xn[part][p], k.half(16, 16))
                if part == 0:
                    wait(dve, L.stat, k.plus(-2).count(N_STAT, 1))
                for t in range(first, last):
                    ins = dve.bn_stats(st[0:NODES, p, t, :], xn[:, p, t, :])
                if part == 1:
                    ins.then_inc(L.bn, 1)

            def stat_math(n, p, c):
                if n == 0:
                    dve.tensor_tensor(ssum[:, c], st[:, p, c, 1], st[:, p, c, 4], ALU.add)
                    dve.tensor_tensor(sdif[:, c], st[:, p, c, 1], st[:, p, c, 4], ALU.subtract)
                    return dve.tensor_tensor(svar[:, c], st[:, p, c, 2], st[:, p, c, 5], ALU.add)
                if n == 1:
                    dve.scalar_tensor_tensor(sd2[:, c], sdif[:, c], 0.25, sdif[:, c], ALU.mult, ALU.mult)
                    return dve.tensor_scalar(sv2[:, c], svar[:, c], 1.0 / D, EPS, ALU.mult, ALU.add)
                if n == 2:
                    return dve.tensor_tensor(var[:, c], sd2[:, c], sv2[:, c], ALU.add)
                if n == 3:
                    return dve.tensor_scalar(guess[:, 0, c], var[:, c].bitcast(I32), -0.5, RSQRT_BITS,
                                             ALU.mult, ALU.add)
                if n == N_STAT:
                    return dve.scalar_tensor_tensor(shift[:, p, c], ssum[:, c], -0.5, rstd[:, p, c],
                                                    ALU.mult, ALU.mult)
                m = (n - 4) // 3
                y = guess[:, m % 2, c].bitcast(F32)
                if (n - 4) % 3 == 0:
                    return dve.tensor_tensor(nwt[:, 0, c], y, y, ALU.mult)
                if (n - 4) % 3 == 1:
                    return dve.scalar_tensor_tensor(nwt[:, 1, c], nwt[:, 0, c], -0.5, var[:, c], ALU.mult, ALU.mult)
                better = guess[:, (m + 1) % 2, c].bitcast(F32) if m < NEWTON - 1 else rstd[:, p, c]
                return dve.scalar_tensor_tensor(better, nwt[:, 1, c], 1.5, y, ALU.add, ALU.mult)

            def stat_step(L, k, n):
                if n == 0:
                    dve.wait_ge(L.bn, k.count(2, 2))
                    wait(dve, L.shift, k.plus(-1).count(1, 1))
                else:
                    dve.wait_ge(L.stat, k.count(N_STAT, n))
                if n == N_STAT - 1:
                    wait(dve, L.relu, k.plus(-2).count(2 * B, 2 * B))
                stat_math(n, k.par, slice(0, 2 * B)).then_inc(L.shift if n == N_STAT else L.stat, 1)

            def all_stats(L, k):
                source_stats(L, k)
                node_stats(L, k, 0)
                node_stats(L, k, 1)
                for n in range(N_STAT + 1):
                    stat_step(L, k, n)

            def segment_max(k):
                p = k.par
                dve.wait_ge(L0.aT, k.count(1, 1))
                wait(dve, L0.maxT, k.plus(-1).count(1, 1))
                dve.tensor_tensor_scan(fmax[:], segm[:, p, 0:WIN], ps_misc[0:BH, 0:WIN], -BIG, ALU.add, ALU.max
                                       ).then_inc(L0.mid, 1)
                dve.wait_ge(L0.mid, k.count(N_MID, 1))
                dve.tensor_tensor_scan(smax[:, ::-1], segm[:, p, 1:WIN + 1][:, ::-1], fmax[:, ::-1], -BIG,
                                       ALU.add, ALU.max).then_inc(L0.mid, 1)

            def below_max(k):
                p = k.par
                dve.wait_ge(L0.maxT, k.count(1, 1))
                wait(dve, L0.exp, k.plus(-1).count(1, 1))
                dve.tensor_tensor(dl[:], alpha[:, p, 0:BH], ps_misc[:, 0:BH], ALU.subtract).then_inc(L0.mid, 1)

            def weigh(k):
                p = k.par
                dve.wait_ge(L0.exp, k.count(1, 1))
                wait(dve, L0.agg, k.plus(-2).count(PAIRS, PAIRS))
                split = dict(h=HEADS)
                dve.tensor_tensor(vw[:, p, :, 0:D].rearrange("e t (h c) -> e t h c", **split),
                                  qkv[:, p, :, 2 * D:3 * D].rearrange("e t (h c) -> e t h c", **split),
                                  vw[:, p, :, D:D + HEADS].unsqueeze(3).to_broadcast([128, B, HEADS, CH]),
                                  ALU.mult).then_inc(L0.mid, 1)

            def pair_scores(k, j):
                p = k.par
                dve.wait_ge(L0.dv, k.count(PAIRS, j + 1))
                dve.wait_ge(L0.qkv_sb, k.count(B, 2 * j + 2))
                wait(dve, L0.tile, k.count(N_TILE, 3 * j))
                t2 = slice(2 * j, 2 * j + 2)
                dve.tensor_tensor(prod[:], ps_dv[:, 2 * D:4 * D].rearrange("e (t c) -> e t c", t=2),
                                  qkv[:, p, t2, D:2 * D], ALU.mult).then_inc(L0.tile, 1)
                if j == 0:
                    wait(dve, L0.added, k.plus(-2).count(1, 1))
                dve.tensor_tensor(xsk[:, p, t2, :], xn[:, p, t2, :],
                                  ps_dv[0:NODES, 0:2 * D].rearrange("e (t c) -> e t c", t=2), ALU.add
                                  ).then_inc(L0.tile, 1)
                dve.wait_ge(L0.tile, k.count(N_TILE, 3 * j + 1))
                if j == 0:
                    wait(dve, L0.mid, k.plus(-2).count(N_MID, 3))
                dve.tensor_reduce(alpha[:, p, 2 * HEADS * j:2 * HEADS * (j + 1)],
                                  prod[:].rearrange("e t (h c) -> e (t h) c", h=HEADS), AX_X, ALU.add
                                  ).then_inc(L0.tile, 1)

            def out_step(k, j, n):
                p = k.par
                t2 = slice(2 * j, 2 * j + 2)
                a = ps_pair[j % 2][0:NODES, 0:2 * (D + 4)].rearrange("n (t c) -> n t c", t=2)
                if n == 0:
                    dve.wait_ge(L0.agg, k.count(PAIRS, j + 1))
                    wait(dve, L0.fin, k.count(N_FIN, (0, 3, 3, 9, 9)[j]))
                else:
                    dve.wait_ge(L0.fin, k.count(N_FIN, fin_count(j, n - 1)))
                if n == 0:
                    ins = dve.tensor_scalar(den[:, j % 2], a[:, :, D:D + HEADS], 1e-16, None, ALU.add)
                elif n == 1:
                    ins = dve.reciprocal(rden[:, j % 2], den[:, j % 2])
                else:
                    if j == 0:
                        wait(dve, L0.stored[p], k.half(16, 0))
                    ins = dve.tensor_tensor(xo[:, p, t2, :].rearrange("n t (h c) -> n t h c", h=HEADS),
                                            a[:, :, 0:D].rearrange("n t (h c) -> n t h c", h=HEADS),
                                            rden[:, j % 2].unsqueeze(3).to_broadcast([NODES, 2, HEADS, CH]), ALU.mult)
                ins.then_inc(L0.fin, 1)

            def step0(k):
                this, prev, nxt, nxt2, nxt3 = (exists(k.plus(n)) for n in (0, -1, 1, 2, 3))

                def outs(*pairs):
                    for n in range(3):
                        for j in pairs:
                            if prev:
                                out_step(k.plus(-1), j, n)

                def stats(*numbers):
                    for n in numbers:
                        if nxt:
                            stat_step(L0, k.plus(1), n)

                if prev:
                    pair_scores(k.plus(-1), PAIRS - 1)
                if nxt:
                    source_stats(L0, k.plus(1), 5, B)
                    node_stats(L0, k.plus(1), 0)
                if prev:
                    segment_max(k.plus(-1))
                if nxt:
                    node_stats(L0, k.plus(1), 1)
                stats(0)
                if prev:
                    below_max(k.plus(-1))
                stats(1)
                if this:
                    pair_scores(k, 0)
                stats(2, 3, 4, 5)
                if prev:
                    weigh(k.plus(-1))
                stats(6, 7, 8, 9)
                if this:
                    pair_scores(k, 1)
                stats(10, 11)
                outs(0)
                stats(12, 13)
                if nxt:
                    segment_mask(k.plus(1))
                if nxt3:
                    idx_rows(k.plus(3))
                outs(1, 2)
                if this:
                    pair_scores(k, 2)
                if nxt:
                    members(L0, k.plus(1), 0, 6, k.plus(-1).count(PAIRS, 3))
                if nxt3:
                    idx_cols(k.plus(3))
                    gather_cols(L0, k.plus(3))
                outs(3, 4)
                if this:
                    pair_scores(k, 3)
                if nxt:
                    members(L0, k.plus(1), 6, B, k.plus(-1).count(PAIRS, PAIRS))
                if nxt2:
                    source_stats(L0, k.plus(2), 0, 5)

            for n in range(2):
                idx_rows(Batch(n))
                idx_cols(Batch(n))
                gather_cols(L0, Batch(n))
            segment_mask(Batch(0))
            idx_rows(Batch(2))
            idx_cols(Batch(2))
            members(L0, Batch(0), 0, 6, 0)
            members(L0, Batch(0), 6, B, 0)
            all_stats(L0, Batch(0))
            gather_cols(L0, Batch(2))
            source_stats(L0, Batch(1), 0, 5)
            list_long_tiles()
            steps(dve, step0, 0, BATCHES)

            def sum_step(k, j, n):
                p, q = k.par, (k.par * PAIRS + j) % 2
                t2 = slice(2 * j, 2 * j + 2)
                a = ps_self[q][0:NODES, 0:2 * D].rearrange("n (t c) -> n t c", t=2)
                m = ps_msg[q][0:NODES, 0:2 * (D + 4)].rearrange("n (t c) -> n t c", t=2)
                if n == 0:
                    dve.wait_ge(L1.qkv, k.count(B, 2 * j + 2))
                    wait(dve, L1.tile, k.count(N_OUT, 3 * j))
                    dve.tensor_tensor(yself[:], xn[:, p, t2, :], a, ALU.add).then_inc(L1.tile, 1)
                elif n == 1:
                    dve.tensor_scalar(deg[:], m[:, :, D:D + 1], 1.0, None, ALU.max).then_inc(L1.tile, 1)
                else:
                    dve.wait_ge(L1.tile, k.count(N_OUT, 3 * j + 2))
                    if j == 0:
                        wait(dve, L1.stored[p], k.half(16, 0))
                    for t in range(2):
                        ins = dve.scalar_tensor_tensor(xo[:, p, 2 * j + t, :], m[:, t, 0:D], deg[:, t, :],
                                                       yself[:, t, :], ALU.mult, ALU.add)
                    ins.then_inc(L1.tile, 1)

            def step1(k):
                nxt, nxt2, nxt3 = (exists(k.plus(n)) for n in (1, 2, 3))

                def sums(j, first):
                    for n in range(3):
                        sum_step(k, j, n)
                        if nxt and first is not None:
                            stat_step(L1, k.plus(1), first + n)

                if nxt:
                    node_stats(L1, k.plus(1), 0)
                sums(0, None)
                if nxt:
                    node_stats(L1, k.plus(1), 1)
                    stat_step(L1, k.plus(1), 0)
                sums(1, 1)
                if nxt:
                    for n in range(4, 9):
                        stat_step(L1, k.plus(1), n)
                    for n in range(9, STAT_STEPS):
                        stat_step(L1, k.plus(1), n)
                if nxt3:
                    gather_cols(L1, k.plus(3))
                sums(2, None)
                if nxt:
                    members(L1, k.plus(1), 0, B, k.plus(-1).count(B, B))
                sums(3, None)
                if nxt2:
                    source_stats(L1, k.plus(2), 0, 5)
                sums(4, None)
                if nxt2:
                    source_stats(L1, k.plus(2), 5, B)

            def long_node_stats(S):
                def before(i, tile, n):
                    base = i * T_DVE[S.n]
                    dve.wait_ge(S.rows, i * 16)
                    dve.bn_stats(st[0:NODES, 0, 0, :], xn[:, 0, 0, :]).then_inc(S.dve_tile, 1)
                    for m in range(STAT_STEPS):
                        dve.wait_ge(S.dve_tile, base + (1 + m))
                        stat_math(m, 0, slice(0, 1)).then_inc(S.dve_tile, 1)
                    dve.memset(acc[:], 0.0).then_inc(S.dve_tile, 1)
                    dve.memset(run_max[:], -BIG).then_inc(S.dve_tile, 1)
                    dve.wait_ge(S.pe_tile, i * T_PE[S.n] + 2)
                    if S is S0:
                        ins = dve.tensor_tensor(xsk[:, 0, 0, :], xn[:, 0, 0, :], ps_dv[0:NODES, 0:D], ALU.add)
                    else:
                        ins = dve.tensor_tensor(yself[:, 0, :], xn[:, 0, 0, :], ps_self[0][0:NODES, 0:D], ALU.add)
                    ins.then_inc(S.dve_tile, 1)
                return before

            def long_members(S, tile, n):
                base = n * C_DVE[S.n]
                dve.wait_ge(S.edges, n * 16)
                dve.tensor_scalar(chunk_d[:], chunk_e[:, 1:2], n0all[0:ROWS, bass.ds(tile, 1)], None, ALU.subtract
                                  ).then_inc(S.dve, 1)
                dve.wait_ge(S.dve, base + 1)
                dve.tensor_scalar(member[0:ROWS, 0, 0, :], iota[0:ROWS, :], chunk_d[:], None, ALU.is_equal
                                  ).then_inc(S.dve, 1)

            def long_source_stats(S, n, first):
                base = n * C_DVE[S.n] + first
                dve.wait_ge(S.gathered, n * 16)
                dve.bn_stats(st[0:ROWS, 0, 1, :], xs[0:ROWS, 0, 0, :]).then_inc(S.dve, 1)
                for m in range(STAT_STEPS):
                    dve.wait_ge(S.dve, base + (1 + m))
                    stat_math(m, 0, slice(1, 2)).then_inc(S.dve, 1)

            def long_chunk0(c, tile, n):
                S, base = S0, n * C_DVE[0] + (STAT_STEPS + 4)
                long_members(S, tile, n)
                dve.wait_ge(S.dve, n * C_DVE[0] + 2)
                dve.tensor_scalar(outside[:], member[0:ROWS, 0, 0, :], -1.0, BIG, ALU.add, ALU.mult).then_inc(S.dve, 1)
                long_source_stats(S, n, 3)
                dve.wait_ge(S.act, n * C_ACT[0] + 3)
                dve.tensor_tensor(prod[0:ROWS, 0, :], ps_dv[0:ROWS, 0:D], qkv[0:ROWS, 0, 0, D:2 * D], ALU.mult
                                  ).then_inc(S.dve, 1)
                dve.wait_ge(S.dve, base + 1)
                dve.tensor_reduce(alpha[0:ROWS, 0, 0:HEADS], prod[0:ROWS, 0, :].rearrange("e (h c) -> e h c", h=HEADS),
                                  AX_X, ALU.add).then_inc(S.dve, 1)
                dve.wait_ge(S.dve, base + 2)
                for h in range(HEADS):
                    ins = dve.scalar_tensor_tensor(masked[:, h, :], member[0:ROWS, 0, 0, :], alpha[0:ROWS, 0, h:h + 1],
                                                   outside[:], ALU.mult, ALU.add)
                ins.then_inc(S.dve, 1)
                dve.wait_ge(S.pe, n * C_PE[0] + 3)
                dve.tensor_reduce(chunk_max[:], ps_agg[0:NODES, 0:HEADS * ROWS].rearrange("n (h e) -> n h e", h=HEADS),
                                  AX_X, ALU.max).then_inc(S.dve, 1)
                dve.wait_ge(S.dve, base + 4)
                dve.tensor_tensor(new_max[:], run_max[:], chunk_max[:], ALU.max).then_inc(S.dve, 1)
                dve.wait_ge(S.dve, base + 5)
                dve.tensor_tensor(max_step[:], run_max[:], new_max[:], ALU.subtract).then_inc(S.dve, 1)
                dve.wait_ge(S.dve, base + 6)
                dve.tensor_copy(run_max[:], new_max[:]).then_inc(S.dve, 1)
                dve.wait_ge(S.pe, n * C_PE[0] + 4)
                dve.tensor_tensor(dl[0:ROWS, 0:HEADS], alpha[0:ROWS, 0, 0:HEADS], ps_misc[0:ROWS, 0:HEADS],
                                  ALU.subtract).then_inc(S.dve, 1)
                dve.wait_ge(S.dve, base + 8)
                dve.tensor_scalar(dl[0:ROWS, 0:HEADS], dl[0:ROWS, 0:HEADS], 0.0, None, ALU.min).then_inc(S.dve, 1)
                dve.wait_ge(S.act, n * C_ACT[0] + 4)
                dve.tensor_tensor(vw[0:ROWS, 0, 0, 0:D].rearrange("e (h c) -> e h c", h=HEADS),
                                  qkv[0:ROWS, 0, 0, 2 * D:3 * D].rearrange("e (h c) -> e h c", h=HEADS),
                                  vw[0:ROWS, 0, 0, D:D + HEADS].unsqueeze(2).to_broadcast([ROWS, HEADS, CH]),
                                  ALU.mult).then_inc(S.dve, 1)
                dve.tensor_tensor(acc[:, 0:D].rearrange("n (h c) -> n h c", h=HEADS),
                                  acc[:, 0:D].rearrange("n (h c) -> n h c", h=HEADS),
                                  rescale[:].unsqueeze(2).to_broadcast([NODES, HEADS, CH]), ALU.mult)
                dve.tensor_tensor(acc[:, D:D + HEADS], acc[:, D:D + HEADS], rescale[:], ALU.mult).then_inc(S.dve, 1)
                dve.wait_ge(S.dve, base + 11)
                dve.wait_ge(S.pe, n * C_PE[0] + 5)
                dve.tensor_tensor(acc[:], acc[:], ps_agg[0:NODES, 0:D + HEADS], ALU.add).then_inc(S.dve, 1)

            def long_finish0(i, tile, n):
                S, base = S0, i * T_DVE[0] + (STAT_STEPS + 4)
                dve.wait_ge(S.dve, n * C_DVE[0])
                dve.tensor_scalar(den[:, 0, 0, :], acc[:, D:D + HEADS], 1e-16, None, ALU.add).then_inc(S.dve_tile, 1)
                dve.wait_ge(S.dve_tile, base + 1)
                dve.reciprocal(rden[:, 0, 0, :], den[:, 0, 0, :]).then_inc(S.dve_tile, 1)
                dve.wait_ge(S.dve_tile, base + 2)
                dve.tensor_tensor(xo[:, 0, 0, :].rearrange("n (h c) -> n h c", h=HEADS),
                                  acc[:, 0:D].rearrange("n (h c) -> n h c", h=HEADS),
                                  rden[:, 0, 0, :].unsqueeze(2).to_broadcast([NODES, HEADS, CH]), ALU.mult
                                  ).then_inc(S.dve_tile, 1)
                dve.wait_ge(S.dve_tile, base + 3)
                dve.tensor_tensor(xo[:, 0, 0, :], xo[:, 0, 0, :], xsk[:, 0, 0, :], ALU.add).then_inc(S.dve_tile, 1)

            def long_chunk1(c, tile, n):
                long_members(S1, tile, n)
                long_source_stats(S1, n, 2)
                dve.wait_ge(S1.pe, n * C_PE[1] + 2)
                dve.tensor_tensor(acc[:], acc[:], ps_msg[0][0:NODES, 0:D + HEADS], ALU.add).then_inc(S1.dve, 1)

            def long_finish1(i, tile, n):
                dve.wait_ge(S1.dve, n * C_DVE[1])
                dve.tensor_scalar(deg[:, 0, :], acc[:, D:D + 1], 1.0, None, ALU.max).then_inc(S1.dve_tile, 1)
                dve.wait_ge(S1.dve_tile, i * T_DVE[1] + (STAT_STEPS + 5))
                dve.scalar_tensor_tensor(xo[:, 0, 0, :], acc[:, 0:D], deg[:, 0, :], yself[:, 0, :],
                                         ALU.mult, ALU.add).then_inc(S1.dve_tile, 1)

            long_tiles(dve, L0, S0, long_node_stats(S0), long_chunk0, long_finish0)
            dve.wait_ge(long_done[0], 1)
            for n in range(2):
                gather_cols(L1, Batch(n))
            members(L1, Batch(0), 0, B, 0)
            all_stats(L1, Batch(0))
            gather_cols(L1, Batch(2))
            source_stats(L1, Batch(1))
            steps(dve, step1, 0, BATCHES - 1)
            long_tiles(dve, L1, S1, long_node_stats(S1), long_chunk1, long_finish1)

        @block.scalar
        def _(act):
            def relu_tile(L, k, j, t, freed_sem, freed):
                p, q, n = k.par, (k.par * PAIRS + j) % 2, 2 * j + t
                if n == 0:
                    act.wait_ge(L.shift, k.count(1, 1))
                wait(act, freed_sem, freed)
                nc.scalar.activation(hn[:, q, t, :], xn[:, p, n, :], ACT.Relu,
                                     scale=rstd[0:NODES, p, n:n + 1], bias=shift[0:NODES, p, n:n + 1]
                                     ).then_inc(L.relu, 1)
                nc.scalar.activation(hs[:, q, t, :], xs[:, p, n, :], ACT.Relu,
                                     scale=rstd[:, p, B + n:B + n + 1], bias=shift[:, p, B + n:B + n + 1]
                                     ).then_inc(L.relu, 1)

            def relu_pair(L, k, j, freed_sem, freed):
                for t in range(2):
                    relu_tile(L, k, j, t, freed_sem, freed)

            def copy_hT(k, j):
                q = (k.par * PAIRS + j) % 2
                act.wait_ge(L0.hT, k.count(PAIRS, j + 1))
                wait(act, L0.dv, k.plus(-1).count(PAIRS, j + 1))
                src = ps_hT[q][:, :].rearrange("c (t s n) -> c t s n", t=2, s=2)
                nc.scalar.copy(hT[:, j, :, 0, 0:NODES], src[:, :, 0, 0:NODES])
                nc.scalar.copy(hT[:, j, :, 1, :], src[:, :, 1, :]).then_inc(L0.hT_sb, 1)

            def copy_qkv(k, j):
                p = k.par
                for t in range(2 * j, 2 * j + 2):
                    act.wait_ge(L0.qkv, k.count(B, t + 1))
                    if t == 0:
                        wait(act, L0.mid, k.plus(-2).count(N_MID, 4))
                    nc.scalar.copy(qkv[:, p, t, :], ps_qkv[t % 2][:, 0:3 * D]).then_inc(L0.qkv_sb, 1)

            def copy_memberT(k, g):
                t, n = 4 * g, min(4, B - 4 * g)
                act.wait_ge(L0.mT, k.count(3, g + 1))
                if g == 0:
                    wait(act, L0.dv, k.plus(-2).count(PAIRS, PAIRS))
                nc.scalar.copy(memberT[:, k.par, t:t + n, :],
                               ps_mT[0:NODES, 0:n * WIN].rearrange("n (t e) -> n t e", e=WIN)).then_inc(L0.mT_sb, 1)

            def exps(k):
                p = k.par
                act.wait_ge(L0.mid, k.count(N_MID, 3))
                wait(act, L0.agg, k.plus(-2).count(PAIRS, PAIRS))
                nc.scalar.activation(vw[:, p, :, D:D + HEADS], dl[:].rearrange("e (t h) -> e t h", h=HEADS),
                                     ACT.Exp, scale=SCALE).then_inc(L0.exp, 1)

            def step0(k):
                this, prev = exists(k), exists(k.plus(-1))
                for j in range(PAIRS):
                    ahead, a = pairs_ahead(k, j + 1)
                    if exists(ahead) and (this or a >= 1):
                        copy_hT(ahead, a)
                    if this and j == 0:
                        copy_memberT(k, 0)
                    ahead, a = pairs_ahead(k, j + 2)
                    if exists(ahead) and (this or a >= 2):
                        relu_pair(L0, ahead, a, L0.hT, ahead.count(PAIRS, a - 1))
                    if this and j == 0:
                        copy_memberT(k, 1)
                    if prev and j == 1:
                        exps(k.plus(-1))
                    if this:
                        copy_qkv(k, j)
                    if this and j == 0:
                        copy_memberT(k, 2)

            act.wait_ge(zeroed, 11)
            relu_pair(L0, Batch(0), 0, L0.hT, 0)
            copy_hT(Batch(0), 0)
            relu_pair(L0, Batch(0), 1, L0.hT, 0)
            steps(act, step0, 0, BATCHES)

            def copy_agg(k, t):
                act.wait_ge(L1.agg, k.count(B, t + 1))
                wait(act, L1.qkv, k.count(B, t - 1))
                nc.scalar.copy(aggT[:, t % 2, :, :],
                               ps_t1[t % 2][:, 0:3 * NODES].rearrange("c (s n) -> c s n", s=3)
                               ).then_inc(L1.hT_sb, 1)

            def step1(k):
                for j in range(PAIRS):
                    for t in range(2):
                        ahead, a = pairs_ahead(k, j + 2)
                        if exists(ahead):
                            relu_tile(L1, ahead, a, t, L1.agg, ahead.count(B, 2 * a - 3 + t))
                        ahead, a = pairs_ahead(k, j + 1)
                        if exists(ahead):
                            copy_agg(ahead, 2 * a + t)

            def long_turned_rows(S):
                def before(i, tile, n):
                    act.wait_ge(S.dve_tile, i * T_DVE[S.n] + (1 + STAT_STEPS))
                    nc.scalar.activation(hn[:, 0, 0, :], xn[:, 0, 0, :], ACT.Relu, scale=rstd[0:NODES, 0, 0:1],
                                         bias=shift[0:NODES, 0, 0:1]).then_inc(S.act_tile, 1)
                    act.wait_ge(S.pe_tile, i * T_PE[S.n] + 1)
                    nc.scalar.copy(hT[:, 0, 0, 0, 0:NODES], ps_hT[0][:, 0:NODES]).then_inc(S.act_tile, 1)
                    if S is S0:
                        act.wait_ge(S.pe_tile, i * T_PE[0] + 2)
                        nc.scalar.copy(qkv[0:NODES, 0, 0, 0:D], ps_qkv[0][0:NODES, 0:D]).then_inc(S.act_tile, 1)
                return before

            def long_relu(S, n):
                act.wait_ge(S.dve, n * C_DVE[S.n] + (STAT_STEPS + 4 - S.n))
                nc.scalar.activation(hs[0:ROWS, 0, 0, :], xs[0:ROWS, 0, 0, :], ACT.Relu, scale=rstd[0:ROWS, 0, 1:2],
                                     bias=shift[0:ROWS, 0, 1:2]).then_inc(S.act, 1)

            def long_chunk0(c, tile, n):
                long_relu(S0, n)
                act.wait_ge(S0.pe, n * C_PE[0] + 1)
                nc.scalar.copy(hT[:, 0, 0, 1, 0:ROWS], ps_hT[0][:, 0:ROWS])
                nc.scalar.copy(memberT[:, 0, 0, 0:ROWS], ps_mT[0:NODES, 0:ROWS]).then_inc(S0.act, 1)
                act.wait_ge(S0.pe, n * C_PE[0] + 2)
                nc.scalar.copy(qkv[0:ROWS, 0, 0, D:3 * D], ps_qkv[1][0:ROWS, 0:2 * D]).then_inc(S0.act, 1)
                act.wait_ge(S0.dve, n * C_DVE[0] + (STAT_STEPS + 4 + 9))
                nc.scalar.activation(rescale[:], max_step[:], ACT.Exp, scale=SCALE)
                nc.scalar.activation(vw[0:ROWS, 0, 0, D:D + HEADS], dl[0:ROWS, 0:HEADS], ACT.Exp, scale=SCALE
                                     ).then_inc(S0.act, 1)

            def long_chunk1(c, tile, n):
                long_relu(S1, n)
                act.wait_ge(S1.pe, n * C_PE[1] + 1)
                nc.scalar.copy(aggT[:, 0, 1:3, :], ps_t1[1][:, 0:2 * NODES].rearrange("c (s n) -> c s n", s=2)
                               ).then_inc(S1.act, 1)

            long_tiles(act, L0, S0, long_turned_rows(S0), long_chunk0, None)
            act.wait_ge(long_done[0], 1)
            relu_pair(L1, Batch(0), 0, L1.agg, 0)
            copy_agg(Batch(0), 0)
            copy_agg(Batch(0), 1)
            relu_pair(L1, Batch(0), 1, L1.agg, 0)
            steps(act, step1, 0, BATCHES - 1)
            long_tiles(act, L1, S1, long_turned_rows(S1), long_chunk1, None)

        @block.tensor
        def _(pe):
            pe.wait_ge(search, 1)
            pe.wait_ge(const_made, 10)
            nc.tensor.matmul(ps_misc[0:ROWS, 0:EROWS], ones[0:1, 0:ROWS], heads_f[:], start=True, stop=True
                             ).then_inc(heads_spread, 1)
            pe.wait_ge(search, 8)
            nc.tensor.transpose(ps_misc[0:2 * TG, 0:ROWS], st_f[:], ident[0:ROWS, 0:ROWS]).then_inc(starts_turned, 1)
            pe.wait_ge(list_step, 3)
            nc.tensor.matmul(ps_mT[0:1, 0:1], falls_any[:], ones[0:ROWS, 0:1], start=True, stop=True
                             ).then_inc(falls_summed, 1)
            pe.wait_ge(bias_placed, 32)
            pe.wait_ge(bias_step, 8)
            pe.wait_ge(const_load, 16 * 12)
            pe.wait_ge(search, 9)
            pe.wait_ge(zeroed, 11)


            def turn_idx(k):
                p = k.par
                pe.wait_ge(L0.idx, k.count(N_IDX, 2))
                if k.known and k.off < 3:
                    wait(pe, L0.idx, k.plus(-1).count(N_IDX, N_IDX))
                wait(pe, L0.seg, k.plus(-2).count(N_SEG, 1))
                pe.sem_inc(L0.small_turn, 1)
                nc.tensor.transpose(ps_misc[:, 0:B], rows_f[:, p, 0, :], ident[0:B, 0:B])
                nc.tensor.transpose(ps_misc[:, B:2 * B], rows_f[:, p, 1, :], ident[0:B, 0:B]
                                    ).then_inc(L0.turned_idx, 1)

            def spread_rows(k):
                wait(pe, L0.mid, k.plus(-2).count(N_MID, 3))
                if k.known and k.off < 2:
                    pe.wait_ge(L0.idx, k.plus(1).count(N_IDX, N_IDX))
                nc.tensor.matmul(ps_misc[0:BH, 0:WIN], rep[:], rows_f[:, k.par, 1, :], start=True, stop=True
                                 ).then_inc(L0.spread, 1)

            def turn_members(k, g):
                p, t = k.par, 4 * g
                if g < 2:
                    pe.wait_ge(L0.member, k.count(2, g + 1))
                wait(pe, L0.mT_sb, k.count(3, g))
                if g == 0:
                    wait(pe, L0.fin, k.plus(-2).count(N_FIN, fin_count(3, 2)))
                for n in range(min(4, B - t)):
                    last = nc.tensor.transpose(ps_mT[0:NODES, n * WIN:(n + 1) * WIN], member[:, p, t + n, :], ident[:])
                last.then_inc(L0.mT, 1)

            def turn_h(k, j):
                q = (k.par * PAIRS + j) % 2
                pe.wait_ge(L0.relu, k.count(2 * B, 4 * j + 4))
                wait(pe, L0.hT_sb, k.count(PAIRS, j - 1))
                out4 = ps_hT[q][:, :].rearrange("c (t s n) -> c t s n", t=2, s=2)
                for t in range(2):
                    nc.tensor.transpose(out4[:, t, 0, 0:NODES], hn[:, q, t, :], ident[0:NODES, 0:NODES])
                    last = nc.tensor.transpose(out4[:, t, 1, :], hs[:, q, t, :], ident[:])
                last.then_inc(L0.hT, 1)

            def project(k, j):
                pe.wait_ge(L0.hT_sb, k.count(PAIRS, j + 1))
                for t in range(2):
                    n = 2 * j + t
                    wait(pe, L0.qkv_sb, k.count(B, n - 1))
                    nc.tensor.matmul(ps_qkv[n % 2][:, 0:D], hT[:, j, t, 0, :], w0[:, 0, :], start=True, stop=False)
                    nc.tensor.matmul(ps_qkv[n % 2][:, 0:D], ones_b[:], bsplit[:, 0:D], start=False, stop=True)
                    kv = ps_qkv[n % 2][:, D:3 * D]
                    nc.tensor.matmul(kv, hT[:, j, t, 1, :], w0[:, 1:3, :].rearrange("c j n -> c (j n)"),
                                     start=True, stop=False)
                    nc.tensor.matmul(kv, ones_b[:], bsplit[:, D:3 * D], start=False, stop=True
                                     ).then_inc(L0.qkv, 1)

            def skip_and_qe(k, j):
                p = k.par
                pe.wait_ge(L0.hT_sb, k.count(PAIRS, j + 1))
                if j == 0:
                    wait(pe, L0.tile, k.plus(-1).count(N_TILE, N_TILE))
                else:
                    pe.wait_ge(L0.tile, k.count(N_TILE, 3 * j - 1))
                for t in range(2):
                    sk = ps_dv[:, t * D:(t + 1) * D]
                    nc.tensor.matmul(sk, hT[:, j, t, 0, :], w0[:, 3, :], start=True, stop=False)
                    nc.tensor.matmul(sk, ones_b[:], bsplit[:, 3 * D:4 * D], start=False, stop=True)
                pe.wait_ge(L0.qkv_sb, k.count(B, 2 * j + 2))
                if j == 0:
                    pe.wait_ge(L0.mT_sb, k.count(3, 3))
                for t in range(2):
                    last = nc.tensor.matmul(ps_dv[:, (2 + t) * D:(3 + t) * D], memberT[:, p, 2 * j + t, :],
                                            qkv[0:NODES, p, 2 * j + t, 0:D], start=True, stop=True)
                last.then_inc(L0.dv, 1)

            def turn_alpha(k):
                pe.wait_ge(L0.tile, k.count(N_TILE, N_TILE))
                if exists(k.plus(3)):
                    pe.wait_ge(L0.idx, k.plus(3).count(N_IDX, N_IDX))
                elif exists(k.plus(1)):
                    pe.wait_ge(L0.seg, k.plus(1).count(N_SEG, 1))
                nc.tensor.transpose(ps_misc[:, 0:WIN], alpha[:, k.par, :], ident[:]).then_inc(L0.aT, 1)

            def turn_max(k):
                pe.wait_ge(L0.mid, k.count(N_MID, 2))
                pe.sem_inc(L0.small_turn, 1)
                nc.tensor.transpose(ps_misc[:, 0:BH], smax[:], ident[0:BH, 0:BH]).then_inc(L0.maxT, 1)

            def aggregate(k, j):
                p = k.par
                pe.wait_ge(L0.mid, k.count(N_MID, 4))
                if j == 1 and exists(k.plus(1)):
                    pe.wait_ge(L0.mT_sb, k.plus(1).count(3, 3))
                wait(pe, L0.fin, k.count(N_FIN, fin_count(j - 2, 2)) if j > 1 else
                     k.plus(-1).count(N_FIN, fin_count((4, 3)[j], 2)))
                for t in range(2):
                    last = nc.tensor.matmul(ps_pair[j % 2][0:NODES, t * (D + 4):(t + 1) * (D + 4)],
                                            member[:, p, 2 * j + t, :], vw[:, p, 2 * j + t, :],
                                            start=True, stop=True)
                last.then_inc(L0.agg, 1)

            def step0(k):
                this, prev = exists(k), exists(k.plus(-1))
                for j in range(PAIRS):
                    ahead, a = pairs_ahead(k, j + 1)
                    if this and exists(ahead):
                        turn_h(ahead, a)
                    if this and j == 0:
                        turn_members(k, 0)
                    if prev and j > 2:
                        aggregate(k.plus(-1), 2 * j - 5)
                    behind, a = pairs_ahead(k, j - 1)
                    if exists(behind) and (this or j == 0):
                        skip_and_qe(behind, a)
                    if prev and j > 2:
                        aggregate(k.plus(-1), 2 * j - 4)
                    if this and j == 0:
                        turn_members(k, 1)
                    if prev and j == 1:
                        turn_max(k.plus(-1))
                    if j == 2 and exists(k.plus(1)):
                        spread_rows(k.plus(1))
                    if this:
                        project(k, j)
                    if this and j == 0:
                        turn_members(k, 2)
                    if prev and j == 2:
                        aggregate(k.plus(-1), 0)
                    if j == 3 and exists(k.plus(3)):
                        turn_idx(k.plus(3))
                    if prev and j == 0:
                        turn_alpha(k.plus(-1))

            for n in range(2):
                turn_idx(Batch(n))
            spread_rows(Batch(0))
            turn_idx(Batch(2))
            turn_h(Batch(0), 0)
            steps(pe, step0, 0, BATCHES)

            def turn_and_sum(k, t):
                p, q = k.par, (k.par * PAIRS + t // 2) % 2
                pe.wait_ge(L1.relu, k.count(2 * B, 2 * t + 2))
                if t == 0:
                    pe.wait_ge(L1.member, k.count(1, 1))
                    pe.wait_ge(L1.ea[p], k.half(16 * B, 16 * B))
                wait(pe, L1.hT_sb, k.count(B, t - 1))
                ps = ps_t1[t % 2]
                nc.tensor.transpose(ps[:, 0:NODES], hn[:, q, t % 2, :], ident[0:NODES, 0:NODES])
                nc.tensor.matmul(ps[:, NODES:2 * NODES], hs[:, q, t % 2, :], member[:, p, t, :], start=True, stop=True)
                nc.tensor.matmul(ps[:, 2 * NODES:3 * NODES], eaw[:, p, t, :], member[:, p, t, :],
                                 start=True, stop=True).then_inc(L1.agg, 1)

            def project1(k, t):
                j, q = t // 2, (k.par * PAIRS + t // 2) % 2
                pe.wait_ge(L1.hT_sb, k.count(B, t + 1))
                if t % 2 == 0:
                    wait(pe, L1.tile, k.count(3 * PAIRS, 3 * (j - 1)))
                a = ps_self[q][0:NODES, (t % 2) * D:(t % 2 + 1) * D]
                nc.tensor.matmul(a, aggT[:, t % 2, 0, :], w1[:, 0:D], start=True, stop=False)
                nc.tensor.matmul(a, ones_b[:, 0:NODES], bsplit[:, 4 * D:5 * D], start=False, stop=True)
                m = ps_msg[q][0:NODES, (t % 2) * (D + 4):(t % 2 + 1) * (D + 4)]
                nc.tensor.matmul(m, aggT[:, t % 2, 1, :], w1m[:], start=True, stop=False)
                nc.tensor.matmul(m, aggT[:, t % 2, 2, :], weaug[:], start=False, stop=True).then_inc(L1.qkv, 1)

            def step1(k):
                for j in range(PAIRS):
                    ahead, a = pairs_ahead(k, j + 1)
                    for t in range(2):
                        project1(k, 2 * j + t)
                        if exists(ahead):
                            turn_and_sum(ahead, 2 * a + t)

            def long_rows_projected(S):
                def before(i, tile, n):
                    pe.wait_ge(S.act_tile, i * T_ACT[S.n] + 1)
                    nc.tensor.transpose(ps_hT[0][:, 0:NODES], hn[:, 0, 0, :], ident[0:NODES, 0:NODES]
                                        ).then_inc(S.pe_tile, 1)
                    pe.wait_ge(S.act_tile, i * T_ACT[S.n] + 2)
                    rows = hT[:, 0, 0, 0, 0:NODES]
                    if S is S0:
                        targets = ((ps_qkv[0], w0[:, 0, :], 0), (ps_dv, w0[:, 3, :], 3 * D))
                    else:
                        targets = ((ps_self[0], w1[:, 0:D], 4 * D),)
                    for to, w, b in targets:
                        nc.tensor.matmul(to[0:NODES, 0:D], rows, w, start=True, stop=False)
                        last = nc.tensor.matmul(to[0:NODES, 0:D], ones_b[:, 0:NODES], bsplit[:, b:b + D],
                                                start=False, stop=True)
                    last.then_inc(S.pe_tile, 1)
                return before

            def long_chunk0(c, tile, n):
                S, dve_base = S0, n * C_DVE[0] + (STAT_STEPS + 4)
                pe.wait_ge(S.act, n * C_ACT[0] + 1)
                nc.tensor.transpose(ps_hT[0][:, 0:ROWS], hs[0:ROWS, 0, 0, :], ident[0:ROWS, 0:ROWS])
                nc.tensor.transpose(ps_mT[0:NODES, 0:ROWS], member[0:ROWS, 0, 0, :], ident[0:ROWS, 0:ROWS]
                                    ).then_inc(S.pe, 1)
                pe.wait_ge(S.act, n * C_ACT[0] + 2)
                kv = ps_qkv[1][0:ROWS, 0:2 * D]
                nc.tensor.matmul(kv, hT[:, 0, 0, 1, 0:ROWS], w0[:, 1:3, :].rearrange("c j n -> c (j n)"),
                                 start=True, stop=False)
                nc.tensor.matmul(kv, ones_b[:, 0:ROWS], bsplit[:, D:3 * D], start=False, stop=True)
                nc.tensor.matmul(ps_dv[0:ROWS, 0:D], memberT[:, 0, 0, 0:ROWS], qkv[0:NODES, 0, 0, 0:D],
                                 start=True, stop=True).then_inc(S.pe, 1)
                pe.wait_ge(S.dve, dve_base + 3)
                for h in range(HEADS):
                    last = nc.tensor.transpose(ps_agg[0:NODES, h * ROWS:(h + 1) * ROWS], masked[:, h, :],
                                               ident[0:ROWS, 0:ROWS])
                last.then_inc(S.pe, 1)
                pe.wait_ge(S.dve, dve_base + 5)
                nc.tensor.matmul(ps_misc[0:ROWS, 0:HEADS], memberT[:, 0, 0, 0:ROWS], new_max[:], start=True, stop=True
                                 ).then_inc(S.pe, 1)
                pe.wait_ge(S.dve, dve_base + 10)
                nc.tensor.matmul(ps_agg[0:NODES, 0:D + HEADS], member[0:ROWS, 0, 0, :], vw[0:ROWS, 0, 0, :],
                                 start=True, stop=True).then_inc(S.pe, 1)

            def long_chunk1(c, tile, n):
                pe.wait_ge(S1.feat, n * 16)
                pe.wait_ge(S1.act, n * C_ACT[1] + 1)
                ps = ps_t1[1]
                nc.tensor.matmul(ps[:, 0:NODES], hs[0:ROWS, 0, 0, :], member[0:ROWS, 0, 0, :], start=True, stop=True)
                nc.tensor.matmul(ps[:, NODES:2 * NODES], eaw[0:ROWS, 0, 0, :], member[0:ROWS, 0, 0, :],
                                 start=True, stop=True).then_inc(S1.pe, 1)
                pe.wait_ge(S1.act, n * C_ACT[1] + 2)
                m = ps_msg[0][0:NODES, 0:D + HEADS]
                nc.tensor.matmul(m, aggT[:, 0, 1, :], w1m[:], start=True, stop=False)
                nc.tensor.matmul(m, aggT[:, 0, 2, :], weaug[:], start=False, stop=True).then_inc(S1.pe, 1)

            long_tiles(pe, L0, S0, long_rows_projected(S0), long_chunk0, None)
            pe.wait_ge(long_done[0], 1)
            turn_and_sum(Batch(0), 0)
            turn_and_sum(Batch(0), 1)
            steps(pe, step1, 0, BATCHES - 1)
            long_tiles(pe, L1, S1, long_rows_projected(S1), long_chunk1, None)


_ORDER = ["x", "edges", "edge_attr_64", "L0_gnn_Wq", "L0_gnn_bq", "L0_gnn_Wk", "L0_gnn_bk", "L0_gnn_Wv", "L0_gnn_bv",
          "L0_gnn_Wskip", "L0_gnn_bskip", "L1_gnn_W_kernel", "L1_gnn_W_bias", "L1_gnn_We_kernel", "L1_gnn_We_bias"]


def kernel(**inputs):
    import concourse.bacc as bacc
    from concourse.bass_utils import run_bass_kernel_spmd

    arrays = {n: np.ascontiguousarray(v) for n, v in inputs.items()}
    arrays["edges"] = np.stack([arrays.pop("src"), arrays.pop("dst")], axis=1)
    nc = bacc.Bacc("TRN2", target_bir_lowering=False, num_devices=1)
    ins = {f"in_{n}": arrays[n] for n in _ORDER}
    args = [nc.dram_tensor(n, a.shape, mybir.dt.from_np(a.dtype), kind="ExternalInput").ap() for n, a in ins.items()]
    out = nc.dram_tensor("out_rows", (N, D), F32, kind="ExternalOutput").ap()
    build(nc, *args, out)
    r = run_bass_kernel_spmd(nc, [ins], core_ids=[0])
    return r.results[0]["out_rows"]
```
